# Optimizing a Trainium2 kernel written in Bass

```python
import numpy as np
import jax
import jax.numpy as jnp

def _softmax(x, axis=-1):
    return jax.nn.softmax(x, axis=axis)

def _gelu(x):
    return jax.nn.gelu(x, approximate=True)

def _silu(x):
    return jax.nn.silu(x)

def _sigmoid(x):
    return jax.nn.sigmoid(x)

def _layernorm(x, axis=-1, eps=1e-05):
    m = jnp.mean(x, axis=axis, keepdims=True)
    v = jnp.var(x, axis=axis, keepdims=True)
    return (x - m) / jnp.sqrt(v + eps)

def _scatter_add(tgt, idx, src, axis=0):
    return tgt.at[idx].add(src)

def _segment_sum(src, seg, n):
    return jax.ops.segment_sum(src, seg, n)
kernel_name = 'mk_seq_postln_d1_jaxref_r8_4a6538'

def setup_inputs(seed: int=0):
    np.random.seed(seed)
    _w = jnp.asarray

    def _L0_attn_setup():
        import jax, jax.numpy as jnp
        import numpy as np
        D_MODEL = 128
        NUM_HEADS = 16
        HEAD_DIM = D_MODEL // NUM_HEADS
        MAX_SEQ_LEN = 256

        def _rope_tables(seq_len, head_dim):
            inv_freq = 1.0 / 10000.0 ** (jnp.arange(0, head_dim, 2, dtype=jnp.float32) / head_dim)
            pos = jnp.arange(seq_len, dtype=jnp.float32)
            freqs = jnp.einsum('i,j->ij', pos, inv_freq)
            return (jnp.cos(freqs), jnp.sin(freqs))

        def _apply_rope(x, cos_half, sin_half):
            x_even = x[..., ::2]
            x_odd = x[..., 1::2]
            rot_even = x_even * cos_half - x_odd * sin_half
            rot_odd = x_even * sin_half + x_odd * cos_half
            return jnp.stack([rot_even, rot_odd], axis=-1).reshape(x.shape)
        key = jax.random.key(seed)
        ks = jax.random.split(key, 9)
        B, S = (2, 256)
        glorot = lambda k: jax.random.normal(k, (D_MODEL, D_MODEL), dtype=jnp.float32) * (1.0 / np.sqrt(D_MODEL))
        return {'x': jax.random.normal(ks[0], (B, S, D_MODEL), dtype=jnp.float32), 'wq': glorot(ks[1]), 'bq': jnp.zeros((D_MODEL,), jnp.float32), 'wk': glorot(ks[2]), 'bk': jnp.zeros((D_MODEL,), jnp.float32), 'wv': glorot(ks[3]), 'bv': jnp.zeros((D_MODEL,), jnp.float32), 'wo': glorot(ks[4]), 'bo': jnp.zeros((D_MODEL,), jnp.float32)}
    _L0_attn_in = _L0_attn_setup()

    def _L0_ffn_setup():
        import jax, jax.numpy as jnp
        import numpy as np
        H = 128
        E = 8
        B, S = (4, 256)
        key = jax.random.key(seed)
        k1, k2, k3, k4 = jax.random.split(key, 4)
        x = jax.random.normal(k1, (B, S, H), dtype=jnp.float32)
        wg = jax.random.normal(k2, (H, E), dtype=jnp.float32) * 0.02
        W = jax.random.normal(k3, (E, H, H), dtype=jnp.float32) * 0.02
        b = jax.random.normal(k4, (E, H), dtype=jnp.float32) * 0.02
        return {'x': x, 'wg': wg, 'W': W, 'b': b}
    _L0_ffn_in = _L0_ffn_setup()
    _d = {'L0_attn_x': _L0_attn_in['x'], 'L0_attn_wq': _L0_attn_in['wq'], 'L0_attn_bq': _L0_attn_in['bq'], 'L0_attn_wk': _L0_attn_in['wk'], 'L0_attn_bk': _L0_attn_in['bk'], 'L0_attn_wv': _L0_attn_in['wv'], 'L0_attn_bv': _L0_attn_in['bv'], 'L0_attn_wo': _L0_attn_in['wo'], 'L0_attn_bo': _L0_attn_in['bo'], 'L0_ffn_wg': _L0_ffn_in['wg'], 'L0_ffn_W': _L0_ffn_in['W'], 'L0_ffn_b': _L0_ffn_in['b']}
    _x0 = _d['L0_attn_x']
    _d['L0_attn_x'] = jax.random.normal(jax.random.fold_in(jax.random.key(seed), 1), (16, 256, 128), dtype=_x0.dtype)
    del _x0
    return _d

def reference(L0_attn_x, L0_attn_wq, L0_attn_bq, L0_attn_wk, L0_attn_bk, L0_attn_wv, L0_attn_bv, L0_attn_wo, L0_attn_bo, L0_ffn_wg, L0_ffn_W, L0_ffn_b):

    def _L0_attn_ref(x, wq, bq, wk, bk, wv, bv, wo, bo):
        import jax, jax.numpy as jnp
        import numpy as np
        D_MODEL = 128
        NUM_HEADS = 16
        HEAD_DIM = D_MODEL // NUM_HEADS
        MAX_SEQ_LEN = 256

        def _rope_tables(seq_len, head_dim):
            inv_freq = 1.0 / 10000.0 ** (jnp.arange(0, head_dim, 2, dtype=jnp.float32) / head_dim)
            pos = jnp.arange(seq_len, dtype=jnp.float32)
            freqs = jnp.einsum('i,j->ij', pos, inv_freq)
            return (jnp.cos(freqs), jnp.sin(freqs))

        def _apply_rope(x, cos_half, sin_half):
            x_even = x[..., ::2]
            x_odd = x[..., 1::2]
            rot_even = x_even * cos_half - x_odd * sin_half
            rot_odd = x_even * sin_half + x_odd * cos_half
            return jnp.stack([rot_even, rot_odd], axis=-1).reshape(x.shape)
        B, S, _ = x.shape
        q = (x @ wq + bq).reshape(B, S, NUM_HEADS, HEAD_DIM)
        k = (x @ wk + bk).reshape(B, S, NUM_HEADS, HEAD_DIM)
        v = (x @ wv + bv).reshape(B, S, NUM_HEADS, HEAD_DIM)
        cos, sin = _rope_tables(S, HEAD_DIM)
        cos = cos[None, :, None, :]
        sin = sin[None, :, None, :]
        q = _apply_rope(q, cos, sin)
        k = _apply_rope(k, cos, sin)
        q = q.transpose(0, 2, 1, 3)
        k = k.transpose(0, 2, 1, 3)
        v = v.transpose(0, 2, 1, 3)
        scores = jnp.einsum('bhqd,bhkd->bhqk', q, k) / jnp.sqrt(jnp.float32(HEAD_DIM))
        causal = jnp.where(jnp.tril(jnp.ones((S, S), jnp.float32)) == 0, -1000000000.0, 0.0)
        scores = scores + causal
        attn = jax.nn.softmax(scores, axis=-1)
        out = jnp.einsum('bhqk,bhkd->bhqd', attn, v)
        out = out.transpose(0, 2, 1, 3).reshape(B, S, D_MODEL)
        return out @ wo + bo

    def _L0_ffn_ref(x, wg, W, b):
        import jax, jax.numpy as jnp
        import numpy as np
        H = 128
        E = 8
        B, S = (4, 256)
        Bb, Ss, Hh = x.shape
        Ee = wg.shape[1]
        T = Bb * Ss
        C = T // Ee
        xt = x.reshape(T, Hh)
        logits = xt @ wg
        probs = jax.nn.softmax(logits, axis=-1)
        idx = jnp.argmax(probs, axis=-1)
        mask = jax.nn.one_hot(idx, Ee, dtype=xt.dtype)
        locations = jnp.cumsum(mask, axis=0) - mask
        mask = mask * (locations < C).astype(xt.dtype)
        gate = jnp.sum(probs * mask, axis=-1)
        loc_s = jnp.sum(locations * mask, axis=-1).astype(jnp.int32)
        loc_oh = jax.nn.one_hot(loc_s, C, dtype=xt.dtype)
        dispatch = mask[:, :, None] * loc_oh[:, None, :]
        combine = gate[:, None, None] * dispatch
        exp_in = jnp.einsum('tec,th->ech', dispatch, xt)
        exp_out = jnp.einsum('ech,efh->ecf', exp_in, W) + b[:, None, :]
        out = jnp.einsum('tec,ecf->tf', combine, exp_out)
        return out.reshape(Bb, Ss, Hh)
    x = L0_attn_x
    x = _layernorm(x + _L0_attn_ref(x, L0_attn_wq, L0_attn_bq, L0_attn_wk, L0_attn_bk, L0_attn_wv, L0_attn_bv, L0_attn_wo, L0_attn_bo), axis=-1)
    x = _layernorm(x + _L0_ffn_ref(x, L0_ffn_wg, L0_ffn_W, L0_ffn_b), axis=-1)
    return x

_drawn_inputs = setup_inputs


def setup_inputs(seed=0):
    import zlib

    import numpy as np

    out = dict(_drawn_inputs(seed))
    spreads = {'L0_attn_bq': (0.0, 0.456),
     'L0_attn_bk': (0.0, 0.573),
     'L0_attn_bv': (0.0, 0.1),
     'L0_attn_bo': (0.0, 0.1)}
    factors = {'L0_ffn_b': 8.0}
    for name, (base, spread) in spreads.items():
        noise = np.random.default_rng([zlib.crc32(name.encode()), seed]).standard_normal(out[name].shape)
        drawn = base * np.exp(spread * noise) if base else spread * noise
        out[name] = jnp.asarray(drawn.astype(out[name].dtype))
    for name, factor in factors.items():
        out[name] = (out[name] * factor).astype(out[name].dtype)
    return out
```

```python
import numpy as np
import concourse.bass as bass
from concourse import mybir
from contextlib import ExitStack

B, S, D = 16, 256, 128
H, HD = 16, 8
E = 8
TOK_TILES = S // 128
CAPACITY = B * S // E
GROUPS, GH = 4, 4
BLK = 32
NBLK = S // BLK
SCORE_ROWS = GH * 3 * HD
EPS = 1e-5
NEG = -3.0e9
BIG = float(2.0 ** 100)
SCALE = float(1.0 / np.sqrt(np.float32(HD)))
V_PITCH, V_ROW = 160, 640
V_WINDOW = [0, 96, 320, 416]

CHUNKS = [[(j, (2 * h, 2 * h + 1))] for j in range(4) for h in range(2)]
CHUNKS += [[(4, (0, 1, 2, 3))], [(5, (0, 1, 2, 3)), (7, (0, 1, 2, 3))], [(6, (0, 1, 2, 3))]]
NCH = len(CHUNKS)
A_SLOT, B_SLOT, PV_SLOT, SLOTS = 0, 2, 3, NCH + 3

CONSTS = {}
def _layout():
    at = 0
    for name, w in (("ident", 128), ("before", 128), ("cos", S), ("sin", S), ("mask_a", BLK), ("mask_b", BLK),
                    ("stacked", BLK), ("head_cols", 128), ("head_is", GH), ("tie", E), ("max_sel", H)):
        CONSTS[name] = (at, w)
        at += w
    return at
NCONST = _layout()


def width(j):
    return S - BLK * j


def parts_of(chunk):
    col, out = 0, []
    for j, groups in chunk:
        for g in groups:
            out.append((j, g, col))
            col += width(j)
    return out


def columns_of(chunk):
    return sum(width(j) * len(gs) for j, gs in chunk)


def layer_kernel(nc, x, wq, bq, wk, bk, wv, bv, wo, bo, wg, W, b, const, expert_rows, out):
    f32, fr, bf = mybir.dt.float32, mybir.dt.float32r, mybir.dt.bfloat16
    ALU, ACT, AX = mybir.AluOpType, mybir.ActivationFunctionType, mybir.AxisListType
    x_t = x.rearrange("b (n p) d -> b p n d", p=128)
    out_t = out.rearrange("b (n p) d -> b p n d", p=128)
    shape = [B, GROUPS, GH, 3, HD, S]
    q_parts, k_parts = (nc.dram_tensor(f"{n}_parts", shape, f32, kind="Internal").ap() for n in "qk")
    q_turned, k_turned = (nc.dram_tensor(f"{n}_turned", shape, f32, kind="Internal").ap() for n in "qk")

    with ExitStack() as ctx:
        def sb(name, shape, dt=f32):
            return ctx.enter_context(nc.sbuf_tensor(name, shape, dt))

        def pb(name, shape):
            return ctx.enter_context(nc.psum_tensor(name, shape, f32))

        def sem(name):
            return ctx.enter_context(nc.semaphore(name))

        cst = sb("cst", [128, NCONST])
        def C(name, rows=slice(0, 128)):
            at, w = CONSTS[name]
            return cst[rows, at:at + w]

        w_in = sb("w_in", [128, 5, 128])
        w_hi, w_lo = sb("w_hi", [128, 5, 128], fr), sb("w_lo", [128, 5, 128], fr)
        bias_rows = sb("bias_rows", [1, 6, 128])
        bias_cols = sb("bias_cols", [128, 5])
        bv_wide = sb("bv_wide", [128, 128])
        wo_plain = sb("wo_plain", [128, 128])
        wo_rows = sb("wo_rows", [128, 2, 128])
        out_bias = sb("out_bias", [128, 128])
        PR = 3
        probs = sb("probs", [128, PR, 512])
        w_exp = probs[:, 0:2, :].rearrange("p a (e f) -> p (a e) f", f=128)
        we_hi, we_lo = sb("we_hi", [128, E, 128], fr), sb("we_lo", [128, E, 128], fr)
        wg_in = sb("wg_in", [128, E])
        wg_hi, wg_lo = sb("wg_hi", [128, E], fr), sb("wg_lo", [128, E], fr)
        rot_cs = sb("rot_cs", [128, 2, 2, S])
        rot_c, rot_s = rot_cs[:, 0], rot_cs[:, 1]
        rows_in = rot_cs[:, :, :, :].rearrange("p a b x -> p (a b x)")
        b_row = sb("b_row", [1, E * 128])
        route_rows = sb("route_rows", [128, E * 128], fr)
        ident_r, mask_a_r, mask_b_r = sb("ident_r", [128, 128], fr), sb("mask_a_r", [128, BLK], fr), sb("mask_b_r", [128, BLK], fr)
        stacked_r = sb("stacked_r", [128, BLK], fr)
        before_bf, ones_bf = sb("before_bf", [128, 128], bf), sb("ones_bf", [128, 128], bf)
        one, minus_half = sb("one", [1, 128]), sb("minus_half", [128, 2])

        x_in = sb("x_in", [128, 2, 128])
        xt_hi = [sb(f"xt_hi{p}", [128, S], fr) for p in range(2)]
        xt_lo = [sb(f"xt_lo{p}", [128, S], fr) for p in range(2)]
        rot = sb("rot", [128, 2, S])
        rot_hi, rot_lo = sb("rot_hi", [128, 2, S], fr), sb("rot_lo", [128, 2, S], fr)
        turn_hi, turn_lo = sb("turn_hi", [128, 2, S], fr), sb("turn_lo", [128, 2, S], fr)
        v_rows = sb("v_rows", [128, 2, 128])
        q_diag = [sb(f"q_diag{p}", [128, GROUPS, GH, S], fr) for p in range(2)]
        k_plain = [sb(f"k_plain{p}", [128, GROUPS, S], fr) for p in range(2)]
        row_max = sb("row_max", [128, NBLK, GROUPS])
        max_wide = sb("max_wide", [128, NBLK, H])
        max_parts = sb("max_parts", [128, NBLK, 128], fr)
        max_rows = sb("max_rows", [32, S], fr)
        v_diag = [sb(f"v_diag{p}", [128, NBLK, V_ROW]) for p in range(2)]
        k_diag = [sb(f"k_diag{p}", [128, GROUPS, GH, S], fr) for p in range(2)]
        q_plain = [sb(f"q_plain{p}", [128, GROUPS, S], fr) for p in range(2)]
        inv_den = sb("inv_den", [128, 2, S])
        attn = sb("attn", [128, 2, S])
        x_res, x_bias = sb("x_res", [128, 2, 128]), sb("x_bias", [128, 2, 128])
        z1, x1, z2 = sb("z1", [128, 2, 128]), sb("x1", [128, 2, 128]), sb("z2", [128, 2, 128])
        y_sel, y_out = sb("y_sel", [128, 2, 128]), sb("y_out", [128, 2, 128])
        st1, mv1, rs1 = sb("st1", [128, 2, 6]), sb("mv1", [128, 2, 2]), sb("rs1", [128, 2])
        st2, mv2, rs2 = sb("st2", [128, 2, 6]), sb("mv2", [128, 2, 2]), sb("rs2", [128, 2])
        x1t_hi, x1t_lo = sb("x1t_hi", [128, S], fr), sb("x1t_lo", [128, S], fr)
        top, below, e_gate = sb("top", [128, 2]), sb("below", [128, 2, E]), sb("e_gate", [128, 2, E])
        e_sum, gate = sb("e_sum", [128, 2]), sb("gate", [128, 2])
        rank, first = sb("rank", [128, 2, E]), sb("first", [128, 2])
        chosen, chosen_f = sb("chosen", [128, 2, E], bf), sb("chosen_f", [128, 2, E])
        seen = sb("seen", [128, E], bf)
        kept, n_kept, gate_kept = sb("kept", [128, 2, E]), sb("n_kept", [128, 2]), sb("gate_kept", [128, 2])
        route = sb("route", [128, S], fr)

        ps_a = [pb(f"ps_a{i}", [128, 512]) for i in range(2)]
        ps_b = [pb(f"ps_b{i}", [128, 512]) for i in range(2)]
        ps_pv = pb("ps_pv", [128, 2, S])
        ps_m = pb("ps_m", [128, 2, 512])
        ps_n = pb("ps_n", [128, 512])
        ps_log = ps_n[:, 0:2 * E].rearrange("p (t e) -> p t e", t=2)
        ps_loc = ps_n[:, 32:32 + 2 * E].rearrange("p (t e) -> p t e", t=2)
        ps_route = ps_n[0:E, 64:64 + S]

        names = """w_loaded c_loaded x_loaded res_loaded parts_written aops_loaded0 aops_loaded1 bops_loaded0 bops_loaded1 maxrows_loaded stored
            xt_ready qk_ready v_ready a_ready b_ready pv_ready y_ready x1t_ready logits_ready loc_ready
            ex_ready moe_ready w_ps_ready
            xh_done exp_done x1h_done egate_done maxrows_done
            a_taken xl_done roped v_done max_done widened parted den_done normed z1_done st1_done mv1_done rs1_done
            x1_done x1l_done top_done below_done gate_sum gate_done rank_done first_done chosen_done kept_done nkept_done
            gk_done route_done moe_taken z2_done st2_done mv2_done rs2_done out_done
            ve1_done ve2_done turnhi_done turnlo_done vrows_done rot_done rothi_done rotlo_done xb_done chosenbf_done seen_done
            ready_dve ready_pool ready_act swapped split_hi w_dve""".split()
        s_ = {n: sem(n) for n in names}

        def after(eng, name, t, per=1, k=0):
            n = t * per + k
            if isinstance(n, int):
                n = min(n, B * per)
                if n <= 0:
                    return
            eng.wait_ge(s_[name], n)

        def of_seq(v, t):
            return v[t] if isinstance(t, int) else v[bass.ds(t, 1)].squeeze(0)

        def diag_block(t, g, j):
            return t[:, g, :, :].rearrange("p h x -> p (h x)")[:, j:GH * S:NBLK]

        def has(t):
            return not isinstance(t, int) or 0 <= t < B

        block = ctx.enter_context(nc.Block())

        def all_steps(eng, step):
            for s in range(-1, 3):
                step(s, s % 2, lambda o: (s + o) // 2)
            with eng.Fori(0, (B - 4) // 2) as u:
                for k in range(2):
                    step(u * 2 + (3 + k), (3 + k) % 2, lambda o: u + (3 + k + o) // 2)
            for s in range(B - 1, B + 2):
                step(s, s % 2, lambda o: (s + o) // 2)

        N_WEIGHT_DMAS = 7 + 5 + 4 + 4

        @block.sync
        def _(sp):
            sp.dma_start(cst[:, :], const).then_inc(s_["c_loaded"], 16)
            w = s_["w_loaded"]
            for i, a in ((0, wq), (2, wk), (4, wv)):
                sp.dma_start(w_in[:, i, :], a).then_inc(w, 16)
            for i, a in ((0, bq), (2, bk), (4, bv), (5, bo)):
                sp.dma_start(bias_rows[:, i, :], a.rearrange("(o n) -> o n", o=1)).then_inc(w, 16)
            sp.dma_start(wo_plain[:, :], wo).then_inc(w, 16)
            sp.dma_start(wg_in[:, :], wg).then_inc(w, 16)
            sp.dma_start(w_exp[:, :, :], W.rearrange("e f h -> f e h")).then_inc(w, 16)
            sp.dma_start(b_row[:, :], b.rearrange("(o e) f -> o (e f)", o=1)).then_inc(w, 16)
            sp.wait_ge(s_["ready_pool"], 1)
            sp.dma_start(rows_in[0:E, :], expert_rows).then_inc(w, 16)
            for gp in range(2):
                for par in range(2):
                    g = 2 * gp + par
                    sp.dma_start(wo_rows[64 * par:64 * par + 32, gp, :], wo[32 * g:32 * g + 32, :]).then_inc(w, 16)

            def step(s, p, half):
                a, b, c, d = s + 1, s, s - 1, s - 2
                q = 1 - p
                if has(d):
                    after(sp, "xb_done", d)
                    sp.dma_start(x_res[:, :, :], of_seq(x_t, d)).then_inc(s_["res_loaded"], 16)
                if has(a):
                    after(sp, "xt_ready", a)
                    sp.dma_start(x_in[:, :, :], of_seq(x_t, a)).then_inc(s_["x_loaded"], 16)
                if has(b):
                    after(sp, "pv_ready", b - 2, NCH, NCH)
                    kp, qp = of_seq(k_turned, b), of_seq(q_parts, b)
                    sp.dma_start(q_plain[p][0:SCORE_ROWS, :, :].bitcast(f32), qp.rearrange("g h t d x -> (h t d) g x"))\
                        .then_inc(s_[f"bops_loaded{p}"], 16)
                    for hl in range(GH):
                        sp.dma_start(k_diag[p][24 * hl:24 * hl + 24, :, hl, :].bitcast(f32),
                                     kp[:, hl].rearrange("g t d x -> (t d) g x")).then_inc(s_[f"bops_loaded{p}"], 16)
                if has(a):
                    for src, name, dsts in ((rot_hi, "rothi_done", ((0, q_parts, 0), (0, q_parts, 2), (1, k_parts, 0), (1, k_parts, 1))),
                                            (rot_lo, "rotlo_done", ((0, q_parts, 1), (1, k_parts, 2))),
                                            (turn_hi, "turnhi_done", ((0, q_turned, 0), (0, q_turned, 2), (1, k_turned, 0), (1, k_turned, 1))),
                                            (turn_lo, "turnlo_done", ((0, q_turned, 1), (1, k_turned, 2)))):
                        after(sp, name, a, 1, 1)
                        for qk, dst, tau in dsts:
                            sp.dma_start(of_seq(dst, a)[:, :, tau].rearrange("g h d x -> (g h) d x"),
                                         src[:, qk, :].bitcast(f32)).then_inc(s_["parts_written"], 16)
                    after(sp, "parts_written", a, 192, 192)
                    qp, kp = of_seq(q_turned, a), of_seq(k_parts, a)
                    after(sp, "a_ready", a - 2, NCH, NCH)
                    sp.dma_start(k_plain[q][0:SCORE_ROWS, :, :].bitcast(f32), kp.rearrange("g h t d x -> (h t d) g x"))\
                        .then_inc(s_[f"aops_loaded{q}"], 16)
                    for hl in range(GH):
                        sp.dma_start(q_diag[q][24 * hl:24 * hl + 24, :, hl, :].bitcast(f32),
                                     qp[:, hl].rearrange("g t d x -> (t d) g x")).then_inc(s_[f"aops_loaded{q}"], 16)
                if has(b):
                    after(sp, "maxrows_done", b, 1, 1)
                    sp.dma_start(q_plain[p][SCORE_ROWS:128, :, :].bitcast(f32),
                                 max_rows[:, :].bitcast(f32).unsqueeze(1).broadcast_to([32, GROUPS, S]))\
                        .then_inc(s_["maxrows_loaded"], 16)
                if has(d):
                    after(sp, "out_done", d, 1, 1)
                    sp.dma_start(of_seq(out_t, d), y_out[:, :, :]).then_inc(s_["stored"], 16)

            all_steps(sp, step)
            sp.wait_ge(s_["stored"], 16 * B)

        @block.gpsimd
        def _(pool):
            def inverse_deviation(mv, rs, n, d):
                after(pool, f"mv{n}_done", d, 2, 2)
                pool.nop(nofuse=True)
                pool.tensor_scalar(rs[:, :], mv[:, :, 1], EPS, None, ALU.add).then_inc(s_[f"ve{n}_done"], 1)
                after(pool, f"ve{n}_done", d, 1, 1)
                pool.tensor_tensor(rs[:, :], rs[:, :], minus_half[:, :], ALU.pow).then_inc(s_[f"rs{n}_done"], 1)

            pool.memset(minus_half[:, :], -0.5)
            pool.memset(wo_rows[:, :, :], 0.0)
            pool.memset(rows_in[:, :], 0.0).then_inc(s_["ready_pool"], 1)
            for p in range(2):
                pool.memset(q_diag[p][:, :, :, :].bitcast(f32), 0.0)
                pool.memset(k_diag[p][:, :, :, :].bitcast(f32), 0.0)
                pool.memset(k_plain[p][:, :, :].bitcast(f32), 0.0)
                pool.memset(q_plain[p][:, :, :].bitcast(f32), 0.0).then_inc(s_["ready_pool"], 1)
            pool.memset(seen[:, :], 0.0).then_inc(s_["ready_pool"], 1)

            def step(s, p, half):
                a, b, c, d = s + 1, s, s - 1, s - 2
                if has(d):
                    after(pool, "res_loaded", d, 16, 16)
                    after(pool, "z1_done", d)
                    pool.tensor_tensor(x_bias[:, :, :], x_res[:, :, :],
                                       out_bias[:, :].unsqueeze(1).broadcast_to([128, 2, 128]), ALU.add)\
                        .then_inc(s_["xb_done"], 1)
                    inverse_deviation(mv1, rs1, 1, d)
                if has(a):
                    after(pool, "roped", a, 1, 1)
                    pool.tensor_tensor(rot[:, :, :], rot_c[:, :, :], rot_s[:, :, :], ALU.add).then_inc(s_["rot_done"], 1)
                    after(pool, "rot_done", a, 1, 1)
                    after(pool, "parts_written", a, 192)
                    pool.nop(nofuse=True)
                    pool.tensor_copy(rot_hi[:, :, :], rot[:, :, :]).then_inc(s_["rothi_done"], 1)
                    after(pool, "rothi_done", a, 1, 1)
                    pool.tensor_tensor(rot_lo[:, :, :], rot[:, :, :], rot_hi[:, :, :].bitcast(f32), ALU.subtract)\
                        .then_inc(s_["rotlo_done"], 1)
                if has(b):
                    after(pool, "vrows_done", b, 1, 1)
                    after(pool, "pv_ready", b - 2, NCH, NCH)
                    if has(a):
                        after(pool, "rotlo_done", a, 1, 1)
                    elif has(d):
                        after(pool, "rs1_done", d, 1, 1)
                    pool.nop(nofuse=True)
                    for jj in range(4):
                        for hl in range(GH):
                            dst = v_diag[p][BLK * hl:BLK * hl + BLK, jj:NBLK:4, :].rearrange("p t (g c) -> p t g c", c=V_PITCH)
                            src = v_rows[BLK * jj:BLK * jj + BLK, :, :].rearrange("p t (g c) -> p t g c", g=GROUPS)
                            last = pool.tensor_copy(dst[:, :, :, HD * hl:HD * hl + HD], src[:, :, :, HD * hl:HD * hl + HD])
                    last.then_inc(s_["v_done"], 1)
                    after(pool, "v_done", b, 1, 1)
                if has(d):
                    after(pool, "loc_ready", d, 1, 1)
                    for t in range(TOK_TILES):
                        pool.tensor_tensor(seen[:, :], seen[:, :], chosen[:, t, :], ALU.add).then_inc(s_["seen_done"], 1)
                        after(pool, "seen_done", d, 2, t + 1)
                    inverse_deviation(mv2, rs2, 2, d)

            pool.wait_ge(s_["w_dve"], 6)
            all_steps(pool, step)

        @block.scalar
        def _(act):
            act.wait_ge(s_["c_loaded"], 16)
            act.wait_ge(s_["ready_pool"], 3)
            for p in range(2):
                for g in range(GROUPS):
                    last = act.activation(
                        k_diag[p][SCORE_ROWS:128, g, :, :],
                        C("max_sel", slice(SCORE_ROWS, 128))[:, GH * g:GH * g + GH].unsqueeze(2).broadcast_to([32, GH, S]),
                        ACT.Copy)
                last.then_inc(s_["ready_act"], 1)

            def step(s, p, half):
                a, b, c, d = s + 1, s, s - 1, s - 2
                q = 1 - p
                for slot in range(SLOTS):
                    if slot == 1 and has(a):
                        after(act, "xt_ready", a, 1, 1)
                        after(act, "v_ready", a - 2, 1, 1)
                        act.activation(xt_hi[q][:, :], ps_m[:, 1, 0:S], ACT.Copy).then_inc(s_["xh_done"], 1)
                    k = slot - B_SLOT
                    if has(c) and 0 <= k < NCH:
                        n = columns_of(CHUNKS[k])
                        after(act, "b_ready", c, NCH, k + 1)
                        after(act, "pv_ready", c, NCH, k + 1 - PR)
                        act.activation(probs[:, k % PR, 0:n], ps_b[k % 2][:, 0:n], ACT.Exp, scale=SCALE)\
                            .then_inc(s_["exp_done"], 1)
                    if slot == 6 and has(d):
                        after(act, "x1t_ready", d, 1, 1)
                        act.activation(x1t_hi[:, :], ps_n[:, 0:S], ACT.Copy).then_inc(s_["x1h_done"], 1)
                    if slot == 8 and has(b):
                        after(act, "v_ready", b, 1, 1)
                        after(act, "v_done", b)
                        act.activation(v_rows[:, :, :], ps_m[:, 0, 0:256].rearrange("p (t c) -> p t c", t=2), ACT.Copy)\
                            .then_inc(s_["vrows_done"], 1)
                    if slot in (7, 9) and has(a):
                        src, dst, n, m = (rot_hi, turn_hi, "rothi_done", "turnhi_done") if slot == 7 else \
                            (rot_lo, turn_lo, "rotlo_done", "turnlo_done")
                        after(act, n, a, 1, 1)
                        after(act, "parts_written", a, 192)
                        act.activation(dst[:, :, :].rearrange("p i (r j) -> p i j r", j=NBLK),
                                       src[:, :, :].bitcast(f32).rearrange("p i (j r) -> p i j r", j=NBLK), ACT.Copy)\
                            .then_inc(s_[m], 1)
                    if slot == 9 and has(d):
                        after(act, "below_done", d, 1, 1)
                        act.activation(e_gate[:, :, :], below[:, :, :], ACT.Exp).then_inc(s_["egate_done"], 1)
                if has(b):
                    after(act, "ex_ready", b, 1, 1)
                    after(act, "maxrows_loaded", b, 16)
                    act.activation(max_rows[:, :], ps_n[0:32, 0:S], ACT.Copy).then_inc(s_["maxrows_done"], 1)

            all_steps(act, step)

        @block.vector
        def _(dve):
            dve.memset(one[:, :], 1.0)
            dve.memset(ones_bf[:, :], 1.0)
            dve.memset(attn[:, :, :], 0.0)
            dve.memset(route[:, :].bitcast(f32), 1.0)
            dve.memset(max_parts[:, :, :].bitcast(f32), 0.0)
            for p in range(2):
                dve.memset(v_diag[p][:, :, :], 0.0).then_inc(s_["ready_dve"], 1)
            dve.wait_ge(s_["ready_dve"], 2)
            dve.wait_ge(s_["c_loaded"], 16)
            for p in range(2):
                for g in range(GROUPS):
                    dve.tensor_copy(v_diag[p][:, :, V_PITCH * g + 32:V_PITCH * g + 64],
                                    C("head_cols")[:, 0:32].unsqueeze(1).broadcast_to([128, NBLK, 32]))
            dve.tensor_copy(ident_r[:, :], C("ident"))
            dve.tensor_copy(mask_a_r[:, :], C("mask_a"))
            dve.tensor_copy(mask_b_r[:, :], C("mask_b"))
            dve.tensor_copy(stacked_r[:, :], C("stacked"))
            dve.tensor_copy(before_bf[:, :], C("before")).then_inc(s_["w_dve"], 1)
            dve.wait_ge(s_["w_loaded"], 16 * 16)
            for i in (0, 2):
                for t, rows in ((w_in, 128), (bias_rows, 1)):
                    src, dst = (t[0:rows, i + o, :].rearrange("p (m two) -> p m two", two=2) for o in (0, 1))
                    dve.tensor_scalar(dst[:, :, 0], src[:, :, 1], -1.0, None, ALU.mult)
                    last = dve.tensor_copy(dst[:, :, 1], src[:, :, 0])
            last.then_inc(s_["swapped"], 1)
            dve.wait_ge(s_["swapped"], 1)
            for hi, full in ((w_hi, w_in), (wg_hi, wg_in)):
                dve.tensor_copy(hi.ap(), full.ap())
            dve.tensor_copy(route_rows[:, :], rows_in[:, :]).then_inc(s_["split_hi"], 1)
            dve.wait_ge(s_["split_hi"], 1)
            dve.tensor_copy(route_rows[32:33, :], b_row[:, :]).then_inc(s_["split_hi"], 1)
            dve.wait_ge(s_["split_hi"], 2)
            dve.tensor_tensor(route_rows[64:65, :], b_row[:, :], route_rows[32:33, :].bitcast(f32), ALU.subtract)
            dve.tensor_tensor(wg_lo[:, :], wg_in[:, :], wg_hi[:, :].bitcast(f32), ALU.subtract)
            dve.tensor_tensor(w_lo[:, :, :], w_in[:, :, :], w_hi[:, :, :].bitcast(f32), ALU.subtract)\
                .then_inc(s_["w_dve"], 1)
            dve.wait_ge(s_["w_ps_ready"], 1)
            dve.tensor_copy(bias_cols[:, :], ps_n[:, 0:5]).then_inc(s_["w_dve"], 1)
            dve.wait_ge(s_["w_dve"], 3)
            dve.tensor_copy(bv_wide[:, :], bias_cols[:, 4:5].broadcast_to([128, 128])).then_inc(s_["w_dve"], 1)
            dve.wait_ge(s_["w_ps_ready"], 2)
            dve.tensor_copy(we_hi[:, :, :], ps_m[:, :, :].rearrange("p a (e f) -> p (a e) f", e=4)).then_inc(s_["w_dve"], 1)
            dve.wait_ge(s_["w_dve"], 5)
            dve.tensor_tensor(we_lo[:, :, :], ps_m[:, :, :].rearrange("p a (e f) -> p (a e) f", e=4),
                              we_hi[:, :, :].bitcast(f32), ALU.subtract)
            dve.wait_ge(s_["w_ps_ready"], 3)
            dve.tensor_copy(out_bias[:, :], ps_n[:, 0:128]).then_inc(s_["w_dve"], 1)

            def norm_stats(z, st, mv, n, d):
                for t in range(2):
                    dve.bn_stats(st[:, t, :], z[:, t, :]).then_inc(s_[f"st{n}_done"], 1)
                for t in range(2):
                    after(dve, f"st{n}_done", d, 2, t + 1)
                    dve.nop(nofuse=True)
                    dve.bn_aggr(mv[:, t, :], st[:, t, :]).then_inc(s_[f"mv{n}_done"], 1)

            def step(s, p, half):
                a, b, c, d = s + 1, s, s - 1, s - 2
                q = 1 - p
                for slot in range(SLOTS):
                    if slot == 0 and has(d):
                        after(dve, "pv_ready", d, NCH, NCH)
                        after(dve, "y_ready", d)
                        dve.reciprocal(inv_den[:, :, :], ps_pv[:, :, :]).then_inc(s_["den_done"], 1)
                        after(dve, "den_done", d, 1, 1)
                        for par in range(2):
                            dve.tensor_tensor(attn[64 * par:64 * par + 32, :, :], ps_pv[64 * par:64 * par + 32, :, :],
                                              inv_den[64 * par + 32:64 * par + 64, :, :], ALU.mult).then_inc(s_["normed"], 1)
                    k = slot - A_SLOT
                    if has(b) and 0 <= k < NCH:
                        after(dve, "a_ready", b, NCH, k + 1)
                        if k == 0:
                            after(dve, "widened", b)
                        col = 0
                        for j, gs in CHUNKS[k]:
                            n = len(gs) * width(j)
                            last = dve.tensor_reduce(row_max[:, NBLK - 1 - j, gs[0]:gs[-1] + 1],
                                                     ps_a[k % 2][:, col:col + n].rearrange("p (g x) -> p g x", g=len(gs)),
                                                     AX.X, ALU.max)
                            col += n
                        last.then_inc(s_["a_taken"], 1)
                    if slot == 1 and has(a):
                        after(dve, "xh_done", a, 1, 1)
                        dve.tensor_tensor(xt_lo[q][:, :], ps_m[:, 1, 0:S], xt_hi[q][:, :].bitcast(f32), ALU.subtract)\
                            .then_inc(s_["xl_done"], 1)
                    if slot == 2 and has(d):
                        after(dve, "y_ready", d, 1, 1)
                        after(dve, "xb_done", d, 1, 1)
                        dve.tensor_tensor(z1[:, :, :], ps_m[:, 0, 0:2 * 128].rearrange("p (t f) -> p t f", t=2),
                                          x_bias[:, :, :], ALU.add).then_inc(s_["z1_done"], 1)
                        after(dve, "z1_done", d, 1, 1)
                        norm_stats(z1, st1, mv1, 1, d)
                    if slot == 3 and has(d):
                        after(dve, "rs1_done", d, 1, 1)
                        for t in range(2):
                            dve.tensor_scalar(x1[:, t, :], z1[:, t, :], mv1[:, t, 0:1], rs1[:, t:t + 1],
                                              ALU.subtract, ALU.mult).then_inc(s_["x1_done"], 1)
                    if slot == 4 and has(a):
                        after(dve, "qk_ready", a, 1, 1)
                        after(dve, "rot_done", a)
                        for i in range(2):
                            dve.scalar_tensor_tensor(out=rot_c[:, i, :], in0=ps_m[:, 0, S * i:S * i + S],
                                                     scalar=bias_cols[:, 2 * i:2 * i + 1], in1=C("cos"),
                                                     op0=ALU.add, op1=ALU.mult)
                            last = dve.scalar_tensor_tensor(out=rot_s[:, i, :], in0=ps_m[:, 1, S * i:S * i + S],
                                                            scalar=bias_cols[:, 2 * i + 1:2 * i + 2], in1=C("sin"),
                                                            op0=ALU.add, op1=ALU.mult)
                        last.then_inc(s_["roped"], 1)
                    if slot == 6 and has(d):
                        after(dve, "x1h_done", d, 1, 1)
                        dve.tensor_tensor(x1t_lo[:, :], ps_n[:, 0:S], x1t_hi[:, :].bitcast(f32), ALU.subtract)\
                            .then_inc(s_["x1l_done"], 1)
                    if slot == 8 and has(d):
                        after(dve, "logits_ready", d, 1, 1)
                        dve.tensor_reduce(top[:, :], ps_log, AX.X, ALU.max).then_inc(s_["top_done"], 1)
                        after(dve, "top_done", d, 1, 1)
                        dve.tensor_tensor(below[:, :, :], ps_log, top[:, :].unsqueeze(2).broadcast_to([128, 2, E]),
                                          ALU.subtract).then_inc(s_["below_done"], 1)
                        after(dve, "below_done", d, 1, 1)
                        dve.scalar_tensor_tensor(out=rank[:, :, :], in0=below[:, :, :], scalar=0.0,
                                                 in1=C("tie").unsqueeze(1).broadcast_to([128, 2, E]),
                                                 op0=ALU.is_ge, op1=ALU.mult).then_inc(s_["rank_done"], 1)
                        after(dve, "rank_done", d, 1, 1)
                        dve.tensor_reduce(first[:, :], rank[:, :, :], AX.X, ALU.max).then_inc(s_["first_done"], 1)
                        after(dve, "first_done", d, 1, 1)
                        after(dve, "seen_done", d, 2)
                        dve.tensor_tensor(chosen[:, :, :], rank[:, :, :], first[:, :].unsqueeze(2).broadcast_to([128, 2, E]),
                                          ALU.is_equal)
                        dve.tensor_tensor(chosen_f[:, :, :], rank[:, :, :], first[:, :].unsqueeze(2).broadcast_to([128, 2, E]),
                                          ALU.is_equal).then_inc(s_["chosen_done"], 1)
                    if slot == 10 and has(d):
                        after(dve, "egate_done", d, 1, 1)
                        dve.tensor_reduce(e_sum[:, :], e_gate[:, :, :], AX.X, ALU.add).then_inc(s_["gate_sum"], 1)
                        after(dve, "gate_sum", d, 1, 1)
                        dve.reciprocal(gate[:, :], e_sum[:, :]).then_inc(s_["gate_done"], 1)
                        after(dve, "loc_ready", d, 1, 1)
                        dve.tensor_scalar(route[0:E, :], ps_route, -1.0, BIG, ALU.add, ALU.mult)
                        dve.scalar_tensor_tensor(out=kept[:, :, :], in0=ps_loc, scalar=float(CAPACITY),
                                                 in1=chosen_f[:, :, :], op0=ALU.is_lt, op1=ALU.mult)\
                            .then_inc(s_["route_done"], 1)
                        after(dve, "route_done", d, 1, 1)
                        dve.tensor_reduce(n_kept[:, :], kept[:, :, :], AX.X, ALU.add).then_inc(s_["nkept_done"], 1)
                        after(dve, "nkept_done", d, 1, 1)
                        dve.tensor_tensor(gate_kept[:, :], n_kept[:, :], gate[:, :], ALU.mult).then_inc(s_["gk_done"], 1)
                    if slot == 11 and has(b):
                        after(dve, "a_taken", b, NCH, NCH)
                        dve.tensor_tensor(max_wide[:, :, :].rearrange("p i (g h) -> p (i g) h", g=GROUPS),
                                          row_max[:, :, :].rearrange("p i g -> p (i g)").unsqueeze(2).broadcast_to([128, NBLK * GROUPS, GH]),
                                          C("head_is").unsqueeze(1).broadcast_to([128, NBLK * GROUPS, GH]), ALU.mult)\
                            .then_inc(s_["widened"], 1)
                        after(dve, "widened", b, 1, 1)
                        dve.tensor_copy(max_parts[:, :, 0:H], max_wide[:, :, :]).then_inc(s_["parted"], 1)
                        after(dve, "parted", b, 2, 1)
                        dve.tensor_tensor(max_parts[:, :, H:2 * H], max_wide[:, :, :], max_parts[:, :, 0:H].bitcast(f32),
                                          ALU.subtract).then_inc(s_["parted"], 1)
                    if slot in (12, 13) and has(d):
                        t = slot - 12
                        after(dve, "moe_ready", d, 2, t + 1)
                        dve.tensor_reduce(y_sel[:, t, :], ps_m[:, :, :].rearrange("p a (e f) -> p f (a e)", e=4),
                                          AX.X, ALU.max).then_inc(s_["moe_taken"], 1)
                        after(dve, "moe_taken", d, 2, t + 1)
                        after(dve, "gk_done", d, 1, 1)
                        dve.scalar_tensor_tensor(out=z2[:, t, :], in0=y_sel[:, t, :], scalar=gate_kept[:, t:t + 1],
                                                 in1=x1[:, t, :], op0=ALU.mult, op1=ALU.add).then_inc(s_["z2_done"], 1)
                if has(d):
                    after(dve, "z2_done", d, 2, 2)
                    norm_stats(z2, st2, mv2, 2, d)
                    after(dve, "rs2_done", d, 1, 1)
                    after(dve, "stored", d, 16)
                    for t in range(2):
                        last = dve.tensor_scalar(y_out[:, t, :], z2[:, t, :], mv2[:, t, 0:1], rs2[:, t:t + 1],
                                                 ALU.subtract, ALU.mult)
                    last.then_inc(s_["out_done"], 1)

            all_steps(dve, step)

        @block.tensor
        def _(pe):
            pe.wait_ge(s_["w_dve"], 2)
            for i in range(5):
                mm = pe.matmul(ps_n[:, i:i + 1], bias_rows[0:1, i, :], one[0:1, 0:1], start=(i == 0), stop=True, skip_group_check=True)
            mm.then_inc(s_["w_ps_ready"], 1)
            for e in range(E):
                mm = pe.transpose(ps_m[:, e // 4, 128 * (e % 4):128 * (e % 4) + 128], w_exp[:, e, :], C("ident"))
            mm.then_inc(s_["w_ps_ready"], 1)
            pe.wait_ge(s_["w_dve"], 4)
            pe.matmul(ps_n[:, 0:128], bv_wide[:, :], wo_plain[:, :], start=True, stop=False)
            pe.matmul(ps_n[:, 0:128], one[0:1, :], bias_rows[0:1, 5, :], start=False, stop=True).then_inc(s_["w_ps_ready"], 1)
            pe.wait_ge(s_["w_dve"], 6)
            pe.wait_ge(s_["ready_pool"], 4)
            pe.wait_ge(s_["ready_act"], 2)
            pe.wait_ge(s_["w_loaded"], 16 * 16)

            def three(out, st, mv, start, stop):
                (sh, sl), (mh, ml) = st, mv
                pe.matmul(out, sh, mh, start=start, stop=False, skip_group_check=True)
                pe.matmul(out, sh, ml, start=False, stop=False, skip_group_check=True)
                return pe.matmul(out, sl, mh, start=False, stop=stop, skip_group_check=True)

            def masks(dst, chunk, rows, at_end):
                col = 0
                for j, gs in chunk:
                    n = len(gs) * width(j)
                    v = dst[:, col:col + n].rearrange("p (g x) -> p g x", g=len(gs))
                    v = v[:, :, width(j) - BLK:width(j)] if at_end else v[:, :, 0:BLK]
                    mm = pe.matmul(v, ident_r[:, :], rows[:, :].unsqueeze(1).broadcast_to([128, len(gs), BLK]),
                                   start=False, stop=True, skip_group_check=True)
                    col += n
                return mm

            def step(s, p, half):
                a, b, c, d = s + 1, s, s - 1, s - 2
                q = 1 - p
                for slot in range(SLOTS):
                    k = slot - B_SLOT
                    if has(c) and 0 <= k < NCH:
                        if k == 0:
                            after(pe, f"bops_loaded{q}", half(-1), 80, 80)
                            after(pe, "maxrows_loaded", c, 16, 16)
                        after(pe, "exp_done", c, NCH, k - 1)
                        for i, (j, g, col) in enumerate(parts_of(CHUNKS[k])):
                            pe.matmul(ps_b[k % 2][:, col:col + width(j)], diag_block(k_diag[q], g, j),
                                      q_plain[q][:, g, BLK * j:S], start=(i == 0), stop=False, skip_group_check=True)
                        masks(ps_b[k % 2], CHUNKS[k], mask_b_r, False).then_inc(s_["b_ready"], 1)
                    k = slot - A_SLOT
                    if has(b) and 0 <= k < NCH:
                        if k == 0:
                            after(pe, f"aops_loaded{p}", half(0), 80, 80)
                        after(pe, "a_taken", b, NCH, k - 1)
                        for i, (j, g, col) in enumerate(parts_of(CHUNKS[k])):
                            pe.matmul(ps_a[k % 2][:, col:col + width(j)], diag_block(q_diag[p], g, NBLK - 1 - j),
                                      k_plain[p][:, g, 0:width(j)], start=(i == 0), stop=False, skip_group_check=True)
                        masks(ps_a[k % 2], CHUNKS[k], mask_a_r, True).then_inc(s_["a_ready"], 1)
                    k = slot - PV_SLOT
                    if has(c) and 0 <= k < NCH:
                        after(pe, "exp_done", c, NCH, k + 1)
                        if k == 0:
                            after(pe, "v_done", c, 1, 1)
                            after(pe, "normed", c, 2)
                        for j, g, col in parts_of(CHUNKS[k]):
                            mm = pe.matmul(ps_pv[:, g // 2, BLK * j:S], v_diag[q][:, j, V_WINDOW[g]:V_WINDOW[g] + 128],
                                           probs[:, k % PR, col:col + width(j)], start=(j == 0 and g == 0),
                                           stop=(k == NCH - 1), skip_group_check=True)
                        mm.then_inc(s_["pv_ready"], 1)
                    if slot == 1 and has(a):
                        after(pe, "x_loaded", a, 16, 16)
                        after(pe, "moe_taken", d - 1, 2, 2)
                        after(pe, "vrows_done", b - 1, 1, 1)
                        for t in range(2):
                            mm = pe.transpose(ps_m[:, 1, 128 * t:128 * t + 128], x_in[:, t, :], C("ident"))
                        mm.then_inc(s_["xt_ready"], 1)
                    if slot == 2 and has(d):
                        after(pe, "moe_taken", d - 1, 2, 2)
                        after(pe, "normed", d, 2, 2)
                        for t in range(2):
                            for gp in range(2):
                                mm = pe.matmul(ps_m[:, 0, 128 * t:128 * t + 128], attn[:, gp, 128 * t:128 * t + 128],
                                               wo_rows[:, gp, :], start=(t == 0 and gp == 0), stop=(gp == 1), skip_group_check=True)
                        mm.then_inc(s_["y_ready"], 1)
                    if slot == 4 and has(a):
                        after(pe, "xl_done", a, 1, 1)
                        if has(d):
                            after(pe, "z1_done", d, 1, 1)
                        for i in range(2):
                            for o in range(2):
                                mm = three(ps_m[:, o, S * i:S * i + S], (w_hi[:, 2 * i + o, :], w_lo[:, 2 * i + o, :]),
                                           (xt_hi[q][:, :], xt_lo[q][:, :]), i == 0, i == 1)
                        mm.then_inc(s_["qk_ready"], 1)
                    if slot == 5 and has(d):
                        after(pe, "x1_done", d, 2, 2)
                        after(pe, "maxrows_done", b)
                        for t in range(2):
                            mm = pe.transpose(ps_n[:, 128 * t:128 * t + 128], x1[:, t, :], C("ident"))
                        mm.then_inc(s_["x1t_ready"], 1)
                    if slot == 6 and has(b):
                        if has(a):
                            after(pe, "roped", a, 1, 1)
                        elif has(d):
                            after(pe, "z1_done", d, 1, 1)
                        for t in range(2):
                            tok = slice(128 * t, 128 * t + 128)
                            mm = three(ps_m[:, 0, tok], (xt_hi[p][:, tok], xt_lo[p][:, tok]),
                                       (w_hi[:, 4, :], w_lo[:, 4, :]), t == 0, t == 1)
                        mm.then_inc(s_["v_ready"], 1)
                    if slot == 7 and has(d):
                        after(pe, "x1l_done", d, 1, 1)
                        for t in range(2):
                            for i, (xa, wb) in enumerate(((x1t_hi, wg_hi), (x1t_hi, wg_lo), (x1t_lo, wg_hi), (x1t_lo, wg_lo))):
                                mm = pe.matmul(ps_log[:, t, :], xa[:, 128 * t:128 * t + 128], wb[:, :],
                                               start=(t == 0 and i == 0), stop=(i == 3), skip_group_check=True)
                        mm.then_inc(s_["logits_ready"], 1)
                    if slot == 9 and has(d):
                        after(pe, "chosen_done", d, 1, 1)
                        after(pe, "seen_done", d, 2)
                        for t in range(2):
                            terms = [(before_bf, chosen[:, t, :]), (ones_bf, seen[:, :])] + [(ones_bf, chosen[:, 0, :])] * t
                            for i, (l, r) in enumerate(terms):
                                pe.matmul(ps_loc[:, t, :], l[:, :], r, start=(t == 0 and i == 0), stop=(i == len(terms) - 1),
                                          skip_group_check=True)
                        for t in range(2):
                            mm = pe.transpose(ps_route[:, 128 * t:128 * t + 128], chosen_f[:, t, :], C("ident"))
                        mm.then_inc(s_["loc_ready"], 1)
                    if slot == 12 and has(b):
                        after(pe, "parted", b, 2, 2)
                        if has(d):
                            after(pe, "route_done", d, 1, 1)
                        for i in range(NBLK):
                            mm = pe.matmul(ps_n[:, BLK * i:BLK * i + BLK], max_parts[:, i, :], stacked_r[:, :],
                                           start=(i == 0), stop=True, skip_group_check=True)
                        mm.then_inc(s_["ex_ready"], 1)
                    if slot in (11, 13) and has(d):
                        t = (slot - 11) // 2
                        if t == 0:
                            if has(b):
                                after(pe, "vrows_done", b, 1, 1)
                        else:
                            after(pe, "moe_taken", d, 2, 1)
                        for h in range(2):
                            o = ps_m[:, h, :].rearrange("p (e f) -> p e f", e=4)
                            tok = slice(128 * t, 128 * t + 128)
                            three(o, (x1t_hi[:, tok], x1t_lo[:, tok]), (we_hi[:, 4 * h:4 * h + 4, :], we_lo[:, 4 * h:4 * h + 4, :]),
                                  True, False)
                            if h == 0:
                                after(pe, "route_done", d, 1, 1)
                            mm = pe.matmul(ps_m[:, h, :], route[:, tok], route_rows[:, 512 * h:512 * h + 512],
                                           start=False, stop=True, skip_group_check=True)
                        mm.then_inc(s_["moe_ready"], 1)

            all_steps(pe, step)


def constants():
    c = np.zeros((128, NCONST), np.float32)
    def put(name, v, rows=slice(0, 128)):
        at, w = CONSTS[name]
        c[rows, at:at + w] = v
    p = np.arange(128)
    put("ident", np.eye(128))
    put("before", (p[:, None] < p[None, :]))
    inv_freq = (np.float32(1) / np.float32(10000) ** (np.arange(0, HD, 2, dtype=np.float32) / np.float32(HD))).astype(np.float32)
    freqs = (np.arange(S, dtype=np.float32)[None, :] * inv_freq[:, None]).astype(np.float32)
    rows = (p % HD) // 2
    put("cos", np.cos(freqs[rows].astype(np.float64)))
    put("sin", np.sin(freqs[rows].astype(np.float64)))
    r, col = p % BLK, np.arange(BLK)
    put("mask_a", np.where(col[None, :] > r[:, None], NEG, 0.0))
    put("mask_b", np.where(col[None, :] < r[:, None], NEG, 0.0))
    put("stacked", r[:, None] == col[None, :])
    put("head_cols", (p[:, None] // BLK) == ((p[None, :] // HD) % GH))
    put("head_is", (p[:, None] // BLK) == np.arange(GH)[None, :])
    put("tie", (E - np.arange(E))[None, :])
    put("max_sel", -((np.arange(32)[:, None] % H) == np.arange(H)[None, :]).astype(np.float32), slice(SCORE_ROWS, 128))
    sel = np.repeat(np.eye(E, dtype=np.float32), 128, axis=1)
    return c, sel


_INS = ['L0_attn_x', 'L0_attn_wq', 'L0_attn_bq', 'L0_attn_wk', 'L0_attn_bk', 'L0_attn_wv', 'L0_attn_bv', 'L0_attn_wo',
        'L0_attn_bo', 'L0_ffn_wg', 'L0_ffn_W', 'L0_ffn_b']


def kernel(**inputs):
    import numpy as _np
    import concourse.bacc as _bacc
    from concourse import mybir as _mybir
    from concourse.bass_utils import run_bass_kernel_spmd as _run

    nc = _bacc.Bacc("TRN2", target_bir_lowering=False, num_devices=1)
    arrays, args = {}, []
    for name in _INS:
        arrays[f"in_{name}_dram"] = _np.ascontiguousarray(inputs[name])
    table, sel = constants()
    arrays["in_table_dram"] = table
    arrays["in_expert_rows_dram"] = sel
    for name, a in arrays.items():
        args.append(nc.dram_tensor(name, a.shape, _mybir.dt.from_np(a.dtype), kind="ExternalInput").ap())
    args.append(nc.dram_tensor("out_0_dram", (B, S, D), _mybir.dt.float32, kind="ExternalOutput").ap())
    layer_kernel(nc, *args)
    r = _run(nc, [arrays], core_ids=[0])
    return r.results[0]["out_0_dram"]
```

```python
import numpy as np
import concourse.bass as bass
from concourse import mybir
from contextlib import ExitStack

B, S, D = 16, 256, 128
H, HD = 16, 8
E = 8
TOK_TILES = S // 128
CAPACITY = B * S // E
GROUPS, GH = 4, 4
BLK = 32
NBLK = S // BLK
SCORE_ROWS = GH * 3 * HD
EPS = 1e-5
NEG = -3.0e9
BIG = float(2.0 ** 100)
SCALE = float(1.0 / np.sqrt(np.float32(HD)))
V_PITCH, V_ROW = 160, 640
V_WINDOW = [0, 96, 320, 416]

CHUNKS = [[(j, (2 * h, 2 * h + 1))] for j in range(4) for h in range(2)]
CHUNKS += [[(4, (0, 1, 2, 3))], [(5, (0, 1, 2, 3)), (7, (0, 1, 2, 3))], [(6, (0, 1, 2, 3))]]
NCH = len(CHUNKS)
B_SLOT, PV_SLOT, SLOTS = 2, 3, NCH + 3
EARLY = 2

CONSTS = {}
def _layout():
    at = 0
    for name, w in (("ident", 128), ("before", 128), ("cos", S), ("sin", S), ("mask_a", BLK), ("mask_b", BLK),
                    ("stacked", BLK), ("head_cols", 128), ("head_is", GH), ("tie", E), ("max_sel", H)):
        CONSTS[name] = (at, w)
        at += w
    return at
NCONST = _layout()


def width(j):
    return S - BLK * j


def parts_of(chunk):
    col, out = 0, []
    for j, groups in chunk:
        for g in groups:
            out.append((j, g, col))
            col += width(j)
    return out


def columns_of(chunk):
    return sum(width(j) * len(gs) for j, gs in chunk)


def layer_kernel(nc, x, wq, bq, wk, bk, wv, bv, wo, bo, wg, W, b, const, expert_rows, out):
    f32, fr, bf = mybir.dt.float32, mybir.dt.float32r, mybir.dt.bfloat16
    ALU, ACT, AX = mybir.AluOpType, mybir.ActivationFunctionType, mybir.AxisListType
    x_t = x.rearrange("b (n p) d -> b p n d", p=128)
    out_t = out.rearrange("b (n p) d -> b p n d", p=128)
    shape = [B, 2, GROUPS, GH, 3, HD, S]
    plain = nc.dram_tensor("plain_parts", shape, f32, kind="Internal").ap()
    turned = nc.dram_tensor("turned_parts", shape, f32, kind="Internal").ap()

    with ExitStack() as ctx:
        def sb(name, shape, dt=f32):
            return ctx.enter_context(nc.sbuf_tensor(name, shape, dt))

        def pb(name, shape):
            return ctx.enter_context(nc.psum_tensor(name, shape, f32))

        def sem(name):
            return ctx.enter_context(nc.semaphore(name))

        cst = sb("cst", [128, NCONST])
        def C(name, rows=slice(0, 128)):
            at, w = CONSTS[name]
            return cst[rows, at:at + w]

        w_in = sb("w_in", [128, 5, 128])
        w_hi, w_lo = sb("w_hi", [128, 5, 128], fr), sb("w_lo", [128, 5, 128], fr)
        bias_rows = sb("bias_rows", [1, 6, 128])
        bias_cols = sb("bias_cols", [128, 5])
        bv_wide = sb("bv_wide", [128, 128])
        wo_in = sb("wo_in", [128, 128])
        out_bias = sb("out_bias", [128, 128])
        PR = 3
        probs = sb("probs", [128, PR, 512])
        w_exp = probs[:, 0:2, :].rearrange("p a (e f) -> p (a e) f", f=128)
        we_hi, we_lo = sb("we_hi", [128, E, 128], fr), sb("we_lo", [128, E, 128], fr)
        wg_in = sb("wg_in", [128, E])
        wg_parts = sb("wg_parts", [128, 2, E], fr)
        rot_cs = sb("rot_cs", [128, 2, 2, S])
        rot_c, rot_s = rot_cs[:, 0], rot_cs[:, 1]
        rows_in = rot_cs[:, :, :, :].rearrange("p a b x -> p (a b x)")
        b_row = sb("b_row", [1, E * 128])
        route_rows = sb("route_rows", [128, E * 128], fr)
        ident_bf, mask_a_bf, mask_b_bf = sb("ident_bf", [128, 128], bf), sb("mask_a_bf", [128, BLK], bf), sb("mask_b_bf", [128, BLK], bf)
        stacked_r = sb("stacked_r", [128, BLK], fr)
        before_bf, ones_bf = sb("before_bf", [128, 128], bf), sb("ones_bf", [128, 128], bf)
        one, minus_half = sb("one", [1, 128]), sb("minus_half", [128, 2])

        x_in = sb("x_in", [128, 2, 128])
        xt_hi = [sb(f"xt_hi{p}", [128, S], fr) for p in range(2)]
        xt_lo = [sb(f"xt_lo{p}", [128, S], fr) for p in range(2)]
        rot = sb("rot", [128, 2, S])
        rot_hi, rot_lo = sb("rot_hi", [128, 2, S], fr), sb("rot_lo", [128, 2, S], fr)
        turn_hi, turn_lo = sb("turn_hi", [128, 2, S], fr), sb("turn_lo", [128, 2, S], fr)
        v_rows = sb("v_rows", [128, 2, 128])
        q_diag = [sb(f"q_diag{p}", [128, GROUPS, GH, S], fr) for p in range(2)]
        k_plain = [sb(f"k_plain{p}", [128, GROUPS, S], fr) for p in range(2)]
        row_max = sb("row_max", [128, NBLK, GROUPS])
        max_wide = sb("max_wide", [128, NBLK, H])
        max_parts = sb("max_parts", [128, NBLK, 2 * H], fr)
        max_rows = sb("max_rows", [32, S], fr)
        v_diag = [sb(f"v_diag{p}", [128, NBLK, V_ROW]) for p in range(2)]
        k_diag = [sb(f"k_diag{p}", [128, GROUPS, GH, S], fr) for p in range(2)]
        q_plain = [sb(f"q_plain{p}", [128, GROUPS, S], fr) for p in range(2)]
        weighted, sums = sb("weighted", [128, S]), sb("sums", [128, S])
        inv_den = sb("inv_den", [128, S])
        attn = sb("attn", [128, S])
        x_res, x_bias = sb("x_res", [128, 2, 128]), sb("x_bias", [128, 2, 128])
        z1, x1, z2 = sb("z1", [128, 2, 128]), sb("x1", [128, 2, 128]), sb("z2", [128, 2, 128])
        y_sel, y_out = sb("y_sel", [128, 2, 128]), sb("y_out", [128, 2, 128])
        st1, mv1, rs1 = sb("st1", [128, 2, 6]), sb("mv1", [128, 2, 2]), sb("rs1", [128, 2])
        st2, mv2, rs2 = sb("st2", [128, 2, 6]), sb("mv2", [128, 2, 2]), sb("rs2", [128, 2])
        x1t_hi, x1t_lo = sb("x1t_hi", [128, S], fr), sb("x1t_lo", [128, S], fr)
        logits = sb("logits", [128, 2, E])
        top, below, e_gate = sb("top", [128, 2]), sb("below", [128, 2, E]), sb("e_gate", [128, 2, E])
        e_sum, gate = sb("e_sum", [128, 2]), sb("gate", [128, 2])
        rank, first = sb("rank", [128, 2, E]), sb("first", [128, 2])
        chosen, chosen_f = sb("chosen", [128, 2, E], bf), sb("chosen_f", [128, 2, E])
        seen = sb("seen", [128, E], bf)
        kept, n_kept, gate_kept = sb("kept", [128, 2, E]), sb("n_kept", [128, 2]), sb("gate_kept", [128, 2])
        route = sb("route", [128, S], fr)

        ps_a = [pb(f"ps_a{i}", [128, 512]) for i in range(2)]
        ps_b = [pb(f"ps_b{i}", [128, 512]) for i in range(2)]
        ps_pv = pb("ps_pv", [128, 2, S])
        ps_m = pb("ps_m", [128, 2, 512])
        ps_n = pb("ps_n", [128, 512])
        ps_log = ps_n[:, 0:4 * E].rearrange("p (t w e) -> p t w e", t=2, w=2)
        ps_loc = ps_n[:, 32:32 + 2 * E].rearrange("p (t e) -> p t e", t=2)
        ps_route = ps_n[0:E, 64:64 + S]

        names = """w_loaded c_loaded x_loaded res_loaded a_parts_written b_parts_written aops_loaded0 aops_loaded1 bops_loaded0 bops_loaded1 maxrows_loaded stored
            xt_ready qk_ready v_ready a_ready b_ready pv_ready y_ready x1t_ready logits_ready loc_ready
            ex_ready moe_ready w_ps_ready
            xh_done exp_done x1h_done egate_done maxrows_done
            a_taken xl_done roped v_done max_done widened parted den_done normed sums_copied pv_copied z1_done st1_done mv1_done rs1_done
            x1_done x1l_done logits_done top_done below_done gate_sum gate_done rank_done first_done chosen_done kept_done nkept_done
            gk_done route_done moe_taken z2_done st2_done mv2_done rs2_done out_done
            ve1_done ve2_done turnhi_done turnlo_done vrows_done rot_done rothi_done rotlo_done xb_done chosenbf_done seen_done
            ready_dve ready_pool ready_act swapped split_hi w_dve""".split()
        s_ = {n: sem(n) for n in names}

        def after(eng, name, t, per=1, k=0):
            n = t * per + k
            if isinstance(n, int):
                n = min(n, B * per)
                if n <= 0:
                    return
            eng.wait_ge(s_[name], n)

        def parts_free(eng, a):
            after(eng, "a_parts_written", a, PARTS_WRITTEN)
            after(eng, "b_parts_written", a, PARTS_WRITTEN)

        def of_seq(v, t):
            return v[t] if isinstance(t, int) else v[bass.ds(t, 1)].squeeze(0)

        def diag_block(t, g, j):
            return t[:, g, :, :].rearrange("p h x -> p (h x)")[:, j:GH * S:NBLK]

        def has(t):
            return not isinstance(t, int) or 0 <= t < B

        def maxima_at(slot, a, b):
            if slot < NCH - EARLY:
                return (b, slot + EARLY) if has(b) else (None, 0)
            if slot >= SLOTS - EARLY:
                return (a, slot - (SLOTS - EARLY)) if has(a) else (None, 0)
            return None, 0

        block = ctx.enter_context(nc.Block())

        def all_steps(eng, step):
            for s in range(-1, 3):
                step(s, s % 2, lambda o: (s + o) // 2)
            with eng.Fori(0, (B - 4) // 2) as u:
                for k in range(2):
                    step(u * 2 + (3 + k), (3 + k) % 2, lambda o: u + (3 + k + o) // 2)
            for s in range(B - 1, B + 2):
                step(s, s % 2, lambda o: (s + o) // 2)

        N_WEIGHT_DMAS = 12
        PARTS_WRITTEN = 6 * 16
        Q_HI, Q_LO, K_HI, K_LO = (0, 1), (2,), (1, 2), (0,)

        @block.sync
        def _(sp):
            sp.dma_start(cst[:, :], const).then_inc(s_["c_loaded"], 16)
            w = s_["w_loaded"]
            for i, a in ((0, wq), (2, wk), (4, wv)):
                sp.dma_start(w_in[:, i, :], a).then_inc(w, 16)
            for i, a in ((0, bq), (2, bk), (4, bv), (5, bo)):
                sp.dma_start(bias_rows[:, i, :], a.rearrange("(o n) -> o n", o=1)).then_inc(w, 16)
            sp.dma_start(wo_in[:, :], wo).then_inc(w, 16)
            sp.dma_start(wg_in[:, :], wg).then_inc(w, 16)
            sp.dma_start(w_exp[:, :, :], W.rearrange("e f h -> f e h")).then_inc(w, 16)
            sp.dma_start(b_row[:, :], b.rearrange("(o e) f -> o (e f)", o=1)).then_inc(w, 16)
            sp.wait_ge(s_["ready_pool"], 1)
            sp.dma_start(rows_in[0:E, :], expert_rows).then_inc(w, 16)

            def step(s, p, half):
                a, b, c, d, e = s + 1, s, s - 1, s - 2, s - 3
                q = 1 - p
                if has(a):
                    after(sp, "xt_ready", a)
                    sp.dma_start(x_in[:, :, :], of_seq(x_t, a)).then_inc(s_["x_loaded"], 16)
                if has(d):
                    after(sp, "xb_done", d)
                    sp.dma_start(x_res[:, :, :], of_seq(x_t, d)).then_inc(s_["res_loaded"], 16)
                if has(b):
                    after(sp, "pv_ready", b - 2, NCH, NCH)
                    after(sp, "b_parts_written", b, PARTS_WRITTEN, PARTS_WRITTEN)
                    sp.nop(nofuse=True)
                    kp, qp = of_seq(turned, b)[1], of_seq(plain, b)[0]
                    sp.dma_start(q_plain[p][0:SCORE_ROWS, :, :].bitcast(f32), qp.rearrange("g h t d x -> (h t d) g x"))\
                        .then_inc(s_[f"bops_loaded{p}"], 16)
                    for hl in range(GH):
                        sp.dma_start(k_diag[p][24 * hl:24 * hl + 24, :, hl, :].bitcast(f32),
                                     kp[:, hl].rearrange("g t d x -> (t d) g x")).then_inc(s_[f"bops_loaded{p}"], 16)
                if has(a):
                    def write(src, dst, qk, taus, name, done):
                        after(sp, done, a, 1, 1)
                        sp.nop(nofuse=True)
                        for tau in taus:
                            sp.dma_start(of_seq(dst, a)[qk, :, :, tau].rearrange("g h d x -> (g h) d x"),
                                         src[:, qk, :].bitcast(f32)).then_inc(s_[name], 16)
                    write(rot_hi, plain, 1, K_HI, "a_parts_written", "rothi_done")
                    write(turn_hi, turned, 0, Q_HI, "a_parts_written", "turnhi_done")
                    write(rot_lo, plain, 1, K_LO, "a_parts_written", "rotlo_done")
                    write(turn_lo, turned, 0, Q_LO, "a_parts_written", "turnlo_done")
                    write(rot_hi, plain, 0, Q_HI, "b_parts_written", "rothi_done")
                    write(rot_lo, plain, 0, Q_LO, "b_parts_written", "rotlo_done")
                    after(sp, "a_parts_written", a, PARTS_WRITTEN, PARTS_WRITTEN)
                    sp.nop(nofuse=True)
                    qp, kp = of_seq(turned, a)[0], of_seq(plain, a)[1]
                    after(sp, "a_ready", a - 2, NCH, NCH)
                    sp.dma_start(k_plain[q][0:SCORE_ROWS, :, :].bitcast(f32), kp.rearrange("g h t d x -> (h t d) g x"))\
                        .then_inc(s_[f"aops_loaded{q}"], 16)
                    for hl in range(GH):
                        sp.dma_start(q_diag[q][24 * hl:24 * hl + 24, :, hl, :].bitcast(f32),
                                     qp[:, hl].rearrange("g t d x -> (t d) g x")).then_inc(s_[f"aops_loaded{q}"], 16)
                    write(turn_hi, turned, 1, K_HI, "b_parts_written", "turnhi_done")
                    write(turn_lo, turned, 1, K_LO, "b_parts_written", "turnlo_done")
                if has(e):
                    after(sp, "out_done", e, 1, 1)
                    sp.nop(nofuse=True)
                    sp.dma_start(of_seq(out_t, e), y_out[:, :, :]).then_inc(s_["stored"], 16)

            all_steps(sp, step)
            after(sp, "out_done", B - 1, 1, 1)
            sp.dma_start(of_seq(out_t, B - 1), y_out[:, :, :]).then_inc(s_["stored"], 16)
            sp.wait_ge(s_["stored"], 16 * B)

        @block.gpsimd
        def _(pool):
            def inverse_deviation(mv, rs, n, d):
                after(pool, f"mv{n}_done", d, 2, 2)
                pool.nop(nofuse=True)
                pool.tensor_scalar(rs[:, :], mv[:, :, 1], EPS, None, ALU.add).then_inc(s_[f"ve{n}_done"], 1)
                after(pool, f"ve{n}_done", d, 1, 1)
                pool.tensor_tensor(rs[:, :], rs[:, :], minus_half[:, :], ALU.pow).then_inc(s_[f"rs{n}_done"], 1)

            def output(e):
                inverse_deviation(mv2, rs2, 2, e)
                after(pool, "rs2_done", e, 1, 1)
                after(pool, "stored", e, 16)
                pool.nop(nofuse=True)
                for t in range(2):
                    last = pool.tensor_scalar(y_out[:, t, :], z2[:, t, :], mv2[:, t, 0:1], rs2[:, t:t + 1],
                                              ALU.subtract, ALU.mult)
                last.then_inc(s_["out_done"], 1)

            pool.memset(minus_half[:, :], -0.5)
            pool.memset(rows_in[:, :], 0.0).then_inc(s_["ready_pool"], 1)
            for p in range(2):
                pool.memset(q_diag[p][:, :, :, :].bitcast(f32), 0.0)
                pool.memset(k_diag[p][:, :, :, :].bitcast(f32), 0.0)
                pool.memset(k_plain[p][:, :, :].bitcast(f32), 0.0)
                pool.memset(q_plain[p][:, :, :].bitcast(f32), 0.0).then_inc(s_["ready_pool"], 1)
            pool.memset(seen[:, :], 0.0).then_inc(s_["ready_pool"], 1)

            def step(s, p, half):
                a, b, c, d, e = s + 1, s, s - 1, s - 2, s - 3
                if has(d):
                    after(pool, "res_loaded", d, 16, 16)
                    after(pool, "z1_done", d)
                    pool.tensor_tensor(x_bias[:, :, :], x_res[:, :, :],
                                       out_bias[:, :].unsqueeze(1).broadcast_to([128, 2, 128]), ALU.add)\
                        .then_inc(s_["xb_done"], 1)
                    inverse_deviation(mv1, rs1, 1, d)
                if has(a):
                    after(pool, "rothi_done", a, 1, 1)
                    parts_free(pool, a)
                    pool.tensor_tensor(rot_lo[:, :, :], rot[:, :, :], rot_hi[:, :, :].bitcast(f32), ALU.subtract)\
                        .then_inc(s_["rotlo_done"], 1)
                if has(b):
                    after(pool, "vrows_done", b, 1, 1)
                    after(pool, "pv_ready", b - 2, NCH, NCH)
                    if has(a):
                        after(pool, "rotlo_done", a, 1, 1)
                    elif has(d):
                        after(pool, "rs1_done", d, 1, 1)
                    pool.nop(nofuse=True)
                    for jj in range(4):
                        for hl in range(GH):
                            dst = v_diag[p][BLK * hl:BLK * hl + BLK, jj:NBLK:4, :].rearrange("p t (g c) -> p t g c", c=V_PITCH)
                            src = v_rows[BLK * jj:BLK * jj + BLK, :, :].rearrange("p t (g c) -> p t g c", g=GROUPS)
                            last = pool.tensor_copy(dst[:, :, :, HD * hl:HD * hl + HD], src[:, :, :, HD * hl:HD * hl + HD])
                    last.then_inc(s_["v_done"], 1)
                    after(pool, "v_done", b, 1, 1)
                if has(e):
                    output(e)
                if has(d):
                    after(pool, "loc_ready", d, 1, 1)
                    for t in range(TOK_TILES):
                        pool.tensor_tensor(seen[:, :], seen[:, :], chosen[:, t, :], ALU.add).then_inc(s_["seen_done"], 1)
                        after(pool, "seen_done", d, 2, t + 1)

            pool.wait_ge(s_["w_dve"], 6)
            all_steps(pool, step)
            output(B - 1)

        @block.scalar
        def _(act):
            act.wait_ge(s_["c_loaded"], 16)
            act.wait_ge(s_["ready_pool"], 3)
            for p in range(2):
                for g in range(GROUPS):
                    last = act.activation(
                        k_diag[p][SCORE_ROWS:128, g, :, :],
                        C("max_sel", slice(SCORE_ROWS, 128))[:, GH * g:GH * g + GH].unsqueeze(2).broadcast_to([32, GH, S]),
                        ACT.Copy)
                last.then_inc(s_["ready_act"], 1)

            def step(s, p, half):
                a, b, c, d = s + 1, s, s - 1, s - 2
                q = 1 - p
                for slot in range(SLOTS):
                    k = slot - B_SLOT
                    if has(c) and 0 <= k < NCH:
                        n = columns_of(CHUNKS[k])
                        after(act, "b_ready", c, NCH, k + 1)
                        after(act, "pv_ready", c, NCH, k + 1 - PR)
                        act.activation(probs[:, k % PR, 0:n], ps_b[k % 2][:, 0:n], ACT.Exp, scale=SCALE)\
                            .then_inc(s_["exp_done"], 1)
                    if slot == 1 and has(a):
                        after(act, "xt_ready", a, 1, 1)
                        after(act, "v_ready", a - 2, 1, 1)
                        act.activation(xt_hi[q][:, :], ps_m[:, 1, 0:S], ACT.Copy).then_inc(s_["xh_done"], 1)
                    if slot == 6 and has(d):
                        after(act, "x1t_ready", d, 1, 1)
                        act.activation(x1t_hi[:, :], ps_n[:, 0:S], ACT.Copy).then_inc(s_["x1h_done"], 1)
                    if slot == 8 and has(b):
                        after(act, "v_ready", b, 1, 1)
                        after(act, "v_done", b)
                        act.activation(v_rows[:, :, :], ps_m[:, 0, 0:256].rearrange("p (t c) -> p t c", t=2), ACT.Copy)\
                            .then_inc(s_["vrows_done"], 1)
                    if slot == 5 and has(a):
                        after(act, "rot_done", a, 1, 1)
                        parts_free(act, a)
                        act.activation(rot_hi[:, :, :], rot[:, :, :], ACT.Copy).then_inc(s_["rothi_done"], 1)
                        act.activation(turn_hi[:, :, :].rearrange("p i (r j) -> p i j r", j=NBLK),
                                       rot[:, :, :].rearrange("p i (j r) -> p i j r", j=NBLK), ACT.Copy)\
                            .then_inc(s_["turnhi_done"], 1)
                    if slot == 6 and has(a):
                        after(act, "rotlo_done", a, 1, 1)
                        act.activation(turn_lo[:, :, :].rearrange("p i (r j) -> p i j r", j=NBLK),
                                       rot_lo[:, :, :].bitcast(f32).rearrange("p i (j r) -> p i j r", j=NBLK), ACT.Copy)\
                            .then_inc(s_["turnlo_done"], 1)
                    if slot == 12 and has(b):
                        after(act, "ex_ready", b, 1, 1)
                        after(act, "maxrows_loaded", b, 16)
                        for i in range(4):
                            last = act.activation(max_rows[:, :].rearrange("m (i2 i r) -> m i i2 r", i2=2, i=4)[:, i],
                                                  ps_n[32 * i:32 * i + 32, 0:2 * BLK].rearrange("m (i2 r) -> m i2 r", i2=2),
                                                  ACT.Copy)
                        last.then_inc(s_["maxrows_done"], 1)
                        after(act, "maxrows_done", b, 1, 1)
                        after(act, "pv_ready", b - 2, NCH, NCH)
                        act.dma_start(q_plain[p][SCORE_ROWS:128, :, :].bitcast(f32),
                                      max_rows[:, :].bitcast(f32).unsqueeze(1).broadcast_to([32, GROUPS, S]))\
                            .then_inc(s_["maxrows_loaded"], 16)
                    if slot == 13 and has(c):
                        after(act, "pv_ready", c, NCH, NCH)
                        after(act, "normed", c)
                        for to, at, done in ((sums, 32, "sums_copied"), (weighted, 0, "pv_copied")):
                            for g in range(GROUPS):
                                rows = 64 * (g % 2) + at
                                last = act.activation(to[32 * g:32 * g + 32, :], ps_pv[rows:rows + 32, g // 2, :], ACT.Copy)
                            last.then_inc(s_[done], 1)
                    if slot == 9 and has(d):
                        after(act, "below_done", d, 1, 1)
                        act.activation(e_gate[:, :, :], below[:, :, :], ACT.Exp).then_inc(s_["egate_done"], 1)
            all_steps(act, step)

        @block.vector
        def _(dve):
            dve.memset(one[:, :], 1.0)
            dve.memset(ones_bf[:, :], 1.0)
            dve.memset(route[:, :].bitcast(f32), 1.0)
            for p in range(2):
                dve.memset(v_diag[p][:, :, :], 0.0).then_inc(s_["ready_dve"], 1)
            dve.wait_ge(s_["ready_dve"], 2)
            dve.wait_ge(s_["c_loaded"], 16)
            for p in range(2):
                for g in range(GROUPS):
                    dve.tensor_copy(v_diag[p][:, :, V_PITCH * g + 32:V_PITCH * g + 64],
                                    C("head_cols")[:, 0:32].unsqueeze(1).broadcast_to([128, NBLK, 32]))
            dve.tensor_copy(ident_bf[:, :], C("ident"))
            dve.tensor_copy(mask_a_bf[:, :], C("mask_a"))
            dve.tensor_copy(mask_b_bf[:, :], C("mask_b"))
            dve.tensor_copy(stacked_r[:, :], C("stacked"))
            dve.tensor_copy(before_bf[:, :], C("before")).then_inc(s_["w_dve"], 1)
            dve.wait_ge(s_["w_loaded"], 16 * N_WEIGHT_DMAS)
            for i in (0, 2):
                for t, rows in ((w_in, 128), (bias_rows, 1)):
                    src, dst = (t[0:rows, i + o, :].rearrange("p (m two) -> p m two", two=2) for o in (0, 1))
                    dve.tensor_scalar(dst[:, :, 0], src[:, :, 1], -1.0, None, ALU.mult)
                    last = dve.tensor_copy(dst[:, :, 1], src[:, :, 0])
            last.then_inc(s_["swapped"], 1)
            dve.wait_ge(s_["swapped"], 1)
            dve.tensor_copy(w_hi[:, :, :], w_in[:, :, :])
            dve.tensor_copy(wg_parts[:, 0, :], wg_in[:, :])
            dve.tensor_copy(route_rows[:, :], rows_in[:, :]).then_inc(s_["split_hi"], 1)
            dve.wait_ge(s_["split_hi"], 1)
            dve.tensor_copy(route_rows[32:33, :], b_row[:, :]).then_inc(s_["split_hi"], 1)
            dve.wait_ge(s_["split_hi"], 2)
            dve.tensor_tensor(route_rows[64:65, :], b_row[:, :], route_rows[32:33, :].bitcast(f32), ALU.subtract)
            dve.tensor_tensor(wg_parts[:, 1, :], wg_in[:, :], wg_parts[:, 0, :].bitcast(f32), ALU.subtract)
            dve.tensor_tensor(w_lo[:, :, :], w_in[:, :, :], w_hi[:, :, :].bitcast(f32), ALU.subtract)\
                .then_inc(s_["w_dve"], 1)
            dve.wait_ge(s_["w_ps_ready"], 1)
            dve.tensor_copy(bias_cols[:, :], ps_n[:, 0:5]).then_inc(s_["w_dve"], 1)
            dve.wait_ge(s_["w_dve"], 3)
            dve.tensor_copy(bv_wide[:, :], bias_cols[:, 4:5].broadcast_to([128, 128])).then_inc(s_["w_dve"], 1)
            dve.wait_ge(s_["w_ps_ready"], 2)
            dve.tensor_copy(we_hi[:, :, :], ps_m[:, :, :].rearrange("p a (e f) -> p (a e) f", e=4)).then_inc(s_["w_dve"], 1)
            dve.wait_ge(s_["w_dve"], 5)
            dve.tensor_tensor(we_lo[:, :, :], ps_m[:, :, :].rearrange("p a (e f) -> p (a e) f", e=4),
                              we_hi[:, :, :].bitcast(f32), ALU.subtract)
            dve.wait_ge(s_["w_ps_ready"], 3)
            dve.tensor_copy(out_bias[:, :], ps_n[:, 0:128]).then_inc(s_["w_dve"], 1)

            def norm_stats(z, st, mv, n, d):
                for t in range(2):
                    dve.bn_stats(st[:, t, :], z[:, t, :]).then_inc(s_[f"st{n}_done"], 1)
                for t in range(2):
                    after(dve, f"st{n}_done", d, 2, t + 1)
                    dve.nop(nofuse=True)
                    dve.bn_aggr(mv[:, t, :], st[:, t, :]).then_inc(s_[f"mv{n}_done"], 1)

            def add_experts(e):
                after(dve, "out_done", e)
                for t in range(2):
                    after(dve, "moe_taken", e, 2, t + 1)
                    after(dve, "gk_done", e, 1, 1)
                    last = dve.scalar_tensor_tensor(out=z2[:, t, :], in0=y_sel[:, t, :], scalar=gate_kept[:, t:t + 1],
                                                    in1=x1[:, t, :], op0=ALU.mult, op1=ALU.add)
                last.then_inc(s_["z2_done"], 1)
                after(dve, "z2_done", e, 1, 1)

            def step(s, p, half):
                a, b, c, d, e = s + 1, s, s - 1, s - 2, s - 3
                q = 1 - p
                for slot in range(SLOTS):
                    t, k = maxima_at(slot, a, b)
                    if t is not None:
                        after(dve, "a_ready", t, NCH, k + 1)
                        if k == 0:
                            after(dve, "widened", t)
                        col = 0
                        for j, gs in CHUNKS[k]:
                            n = len(gs) * width(j)
                            last = dve.tensor_reduce(row_max[:, NBLK - 1 - j, gs[0]:gs[-1] + 1],
                                                     ps_a[k % 2][:, col:col + n].rearrange("p (g x) -> p g x", g=len(gs)),
                                                     AX.X, ALU.max)
                            col += n
                        last.then_inc(s_["a_taken"], 1)
                    if slot == 0 and has(d):
                        after(dve, "sums_copied", d, 1, 1)
                        dve.reciprocal(inv_den[:, :], sums[:, :]).then_inc(s_["den_done"], 1)
                    if slot == 1 and has(d):
                        after(dve, "pv_copied", d, 1, 1)
                        after(dve, "y_ready", d)
                        after(dve, "den_done", d, 1, 1)
                        dve.tensor_tensor(attn[:, :], weighted[:, :], inv_den[:, :], ALU.mult).then_inc(s_["normed"], 1)
                    if slot == 3 and has(e):
                        add_experts(e)
                    if slot == 6 and has(e):
                        norm_stats(z2, st2, mv2, 2, e)
                    if slot == 1 and has(a):
                        after(dve, "xh_done", a, 1, 1)
                        dve.tensor_tensor(xt_lo[q][:, :], ps_m[:, 1, 0:S], xt_hi[q][:, :].bitcast(f32), ALU.subtract)\
                            .then_inc(s_["xl_done"], 1)
                    if slot == 3 and has(d):
                        after(dve, "y_ready", d, 1, 1)
                        after(dve, "xb_done", d, 1, 1)
                        dve.tensor_tensor(z1[:, :, :], ps_n[:, 0:2 * 128].rearrange("p (t f) -> p t f", t=2),
                                          x_bias[:, :, :], ALU.add).then_inc(s_["z1_done"], 1)
                        after(dve, "z1_done", d, 1, 1)
                        norm_stats(z1, st1, mv1, 1, d)
                    if slot == 5 and has(d):
                        after(dve, "rs1_done", d, 1, 1)
                        for t in range(2):
                            dve.tensor_scalar(x1[:, t, :], z1[:, t, :], mv1[:, t, 0:1], rs1[:, t:t + 1],
                                              ALU.subtract, ALU.mult).then_inc(s_["x1_done"], 1)
                    if slot == 4 and has(a):
                        after(dve, "qk_ready", a, 1, 1)
                        for i in range(2):
                            dve.scalar_tensor_tensor(out=rot_c[:, i, :], in0=ps_m[:, 0, S * i:S * i + S],
                                                     scalar=bias_cols[:, 2 * i:2 * i + 1], in1=C("cos"),
                                                     op0=ALU.add, op1=ALU.mult)
                            last = dve.scalar_tensor_tensor(out=rot_s[:, i, :], in0=ps_m[:, 1, S * i:S * i + S],
                                                            scalar=bias_cols[:, 2 * i + 1:2 * i + 2], in1=C("sin"),
                                                            op0=ALU.add, op1=ALU.mult)
                        last.then_inc(s_["roped"], 1)
                        after(dve, "roped", a, 1, 1)
                        after(dve, "rotlo_done", a)
                        after(dve, "turnhi_done", a)
                        dve.tensor_tensor(rot[:, :, :], rot_c[:, :, :], rot_s[:, :, :], ALU.add).then_inc(s_["rot_done"], 1)
                    if slot == 7 and has(d):
                        after(dve, "x1h_done", d, 1, 1)
                        dve.tensor_tensor(x1t_lo[:, :], ps_n[:, 0:S], x1t_hi[:, :].bitcast(f32), ALU.subtract)\
                            .then_inc(s_["x1l_done"], 1)
                    if slot == 8 and has(d):
                        after(dve, "logits_ready", d, 1, 1)
                        dve.tensor_reduce(logits[:, :, :], ps_log.rearrange("p t w e -> p t e w"), AX.X, ALU.add)\
                            .then_inc(s_["logits_done"], 1)
                        after(dve, "logits_done", d, 1, 1)
                        dve.tensor_reduce(top[:, :], logits[:, :, :], AX.X, ALU.max).then_inc(s_["top_done"], 1)
                        after(dve, "top_done", d, 1, 1)
                        dve.tensor_tensor(below[:, :, :], logits[:, :, :], top[:, :].unsqueeze(2).broadcast_to([128, 2, E]),
                                          ALU.subtract).then_inc(s_["below_done"], 1)
                        after(dve, "below_done", d, 1, 1)
                        dve.scalar_tensor_tensor(out=rank[:, :, :], in0=below[:, :, :], scalar=0.0,
                                                 in1=C("tie").unsqueeze(1).broadcast_to([128, 2, E]),
                                                 op0=ALU.is_ge, op1=ALU.mult).then_inc(s_["rank_done"], 1)
                        after(dve, "rank_done", d, 1, 1)
                        dve.tensor_reduce(first[:, :], rank[:, :, :], AX.X, ALU.max).then_inc(s_["first_done"], 1)
                        after(dve, "first_done", d, 1, 1)
                        after(dve, "seen_done", d, 2)
                        dve.tensor_tensor(chosen[:, :, :], rank[:, :, :], first[:, :].unsqueeze(2).broadcast_to([128, 2, E]),
                                          ALU.is_equal)
                        dve.tensor_tensor(chosen_f[:, :, :], rank[:, :, :], first[:, :].unsqueeze(2).broadcast_to([128, 2, E]),
                                          ALU.is_equal).then_inc(s_["chosen_done"], 1)
                    if slot == 10 and has(d):
                        after(dve, "egate_done", d, 1, 1)
                        dve.tensor_reduce(e_sum[:, :], e_gate[:, :, :], AX.X, ALU.add).then_inc(s_["gate_sum"], 1)
                        after(dve, "gate_sum", d, 1, 1)
                        dve.reciprocal(gate[:, :], e_sum[:, :]).then_inc(s_["gate_done"], 1)
                        after(dve, "loc_ready", d, 1, 1)
                        dve.tensor_scalar(route[0:E, :], ps_route, -1.0, BIG, ALU.add, ALU.mult)
                        dve.scalar_tensor_tensor(out=kept[:, :, :], in0=ps_loc, scalar=float(CAPACITY),
                                                 in1=chosen_f[:, :, :], op0=ALU.is_lt, op1=ALU.mult)\
                            .then_inc(s_["route_done"], 1)
                        after(dve, "route_done", d, 1, 1)
                        dve.tensor_reduce(n_kept[:, :], kept[:, :, :], AX.X, ALU.add).then_inc(s_["nkept_done"], 1)
                        after(dve, "nkept_done", d, 1, 1)
                        dve.tensor_tensor(gate_kept[:, :], n_kept[:, :], gate[:, :], ALU.mult).then_inc(s_["gk_done"], 1)
                    if slot == 9 and has(b):
                        after(dve, "a_taken", b, NCH, NCH)
                        dve.tensor_tensor(max_wide[:, :, :].rearrange("p i (g h) -> p (i g) h", g=GROUPS),
                                          row_max[:, :, :].rearrange("p i g -> p (i g)").unsqueeze(2).broadcast_to([128, NBLK * GROUPS, GH]),
                                          C("head_is").unsqueeze(1).broadcast_to([128, NBLK * GROUPS, GH]), ALU.mult)\
                            .then_inc(s_["widened"], 1)
                        after(dve, "widened", b, 1, 1)
                        dve.tensor_copy(max_parts[:, :, 0:H], max_wide[:, :, :]).then_inc(s_["parted"], 1)
                        after(dve, "parted", b, 2, 1)
                        dve.tensor_tensor(max_parts[:, :, H:2 * H], max_wide[:, :, :], max_parts[:, :, 0:H].bitcast(f32),
                                          ALU.subtract).then_inc(s_["parted"], 1)
                    if slot in (12, 13) and has(d):
                        t = slot - 12
                        after(dve, "moe_ready", d, 2, t + 1)
                        dve.tensor_reduce(y_sel[:, t, :], ps_m[:, :, :].rearrange("p a (e f) -> p f (a e)", e=4),
                                          AX.X, ALU.max).then_inc(s_["moe_taken"], 1)

            all_steps(dve, step)
            add_experts(B - 1)
            norm_stats(z2, st2, mv2, 2, B - 1)

        @block.tensor
        def _(pe):
            pe.wait_ge(s_["w_dve"], 2)
            for i in range(5):
                mm = pe.matmul(ps_n[:, i:i + 1], bias_rows[0:1, i, :], one[0:1, 0:1], start=(i == 0), stop=True, skip_group_check=True)
            mm.then_inc(s_["w_ps_ready"], 1)
            for e in range(E):
                mm = pe.transpose(ps_m[:, e // 4, 128 * (e % 4):128 * (e % 4) + 128], w_exp[:, e, :], C("ident"))
            mm.then_inc(s_["w_ps_ready"], 1)
            pe.wait_ge(s_["w_dve"], 4)
            pe.matmul(ps_n[:, 0:128], bv_wide[:, :], wo_in[:, :], start=True, stop=False)
            pe.matmul(ps_n[:, 0:128], one[0:1, :], bias_rows[0:1, 5, :], start=False, stop=True).then_inc(s_["w_ps_ready"], 1)
            pe.wait_ge(s_["w_dve"], 6)
            pe.wait_ge(s_["ready_pool"], 4)
            pe.wait_ge(s_["ready_act"], 2)
            pe.wait_ge(s_["w_loaded"], 16 * N_WEIGHT_DMAS)

            def three(out, st, mv, start, stop):
                (sh, sl), (mh, ml) = st, mv
                pe.matmul(out, sh, mh, start=start, stop=False, skip_group_check=True)
                pe.matmul(out, sh, ml, start=False, stop=False, skip_group_check=True)
                return pe.matmul(out, sl, mh, start=False, stop=stop, skip_group_check=True)

            def masks(dst, chunk, rows, at_end):
                col = 0
                for j, gs in chunk:
                    n = len(gs) * width(j)
                    v = dst[:, col:col + n].rearrange("p (g x) -> p g x", g=len(gs))
                    v = v[:, :, width(j) - BLK:width(j)] if at_end else v[:, :, 0:BLK]
                    mm = pe.matmul(v, ident_bf[:, :], rows[:, :].unsqueeze(1).broadcast_to([128, len(gs), BLK]),
                                   start=False, stop=True, skip_group_check=True)
                    col += n
                return mm

            def step(s, p, half):
                a, b, c, d = s + 1, s, s - 1, s - 2
                q = 1 - p
                for slot in range(SLOTS):
                    k = slot - B_SLOT
                    if has(c) and 0 <= k < NCH:
                        if k == 0:
                            after(pe, f"bops_loaded{q}", half(-1), 80, 80)
                            after(pe, "maxrows_loaded", c, 16, 16)
                        after(pe, "exp_done", c, NCH, k - 1)
                        for i, (j, g, col) in enumerate(parts_of(CHUNKS[k])):
                            pe.matmul(ps_b[k % 2][:, col:col + width(j)], diag_block(k_diag[q], g, j),
                                      q_plain[q][:, g, BLK * j:S], start=(i == 0), stop=False, skip_group_check=True)
                        masks(ps_b[k % 2], CHUNKS[k], mask_b_bf, False).then_inc(s_["b_ready"], 1)
                    t, k = maxima_at(slot, a, b)
                    if t is not None:
                        at = p if t is b else q
                        if k == 0:
                            after(pe, f"aops_loaded{at}", half(0 if t is b else 1), 80, 80)
                        after(pe, "a_taken", t, NCH, max(k - 1, 0))
                        for i, (j, g, col) in enumerate(parts_of(CHUNKS[k])):
                            pe.matmul(ps_a[k % 2][:, col:col + width(j)], diag_block(q_diag[at], g, NBLK - 1 - j),
                                      k_plain[at][:, g, 0:width(j)], start=(i == 0), stop=False, skip_group_check=True)
                        masks(ps_a[k % 2], CHUNKS[k], mask_a_bf, True).then_inc(s_["a_ready"], 1)
                    k = slot - PV_SLOT
                    if has(c) and 0 <= k < NCH:
                        after(pe, "exp_done", c, NCH, k + 1)
                        if k == 0:
                            after(pe, "v_done", c, 1, 1)
                            after(pe, "pv_copied", c)
                        for j, g, col in parts_of(CHUNKS[k]):
                            mm = pe.matmul(ps_pv[:, g // 2, BLK * j:S], v_diag[q][:, j, V_WINDOW[g]:V_WINDOW[g] + 128],
                                           probs[:, k % PR, col:col + width(j)], start=(j == 0 and g == 0),
                                           stop=(k == NCH - 1), skip_group_check=True)
                        mm.then_inc(s_["pv_ready"], 1)
                    if slot == 1 and has(a):
                        after(pe, "x_loaded", a, 16, 16)
                        after(pe, "moe_taken", d - 1, 2, 2)
                        after(pe, "vrows_done", b - 1, 1, 1)
                        for t in range(2):
                            mm = pe.transpose(ps_m[:, 1, 128 * t:128 * t + 128], x_in[:, t, :], C("ident"))
                        mm.then_inc(s_["xt_ready"], 1)
                    if slot == 3 and has(a):
                        after(pe, "xl_done", a, 1, 1)
                        for i in range(2):
                            for o in range(2):
                                mm = three(ps_m[:, o, S * i:S * i + S], (w_hi[:, 2 * i + o, :], w_lo[:, 2 * i + o, :]),
                                           (xt_hi[q][:, :], xt_lo[q][:, :]), i == 0, i == 1)
                        mm.then_inc(s_["qk_ready"], 1)
                    if slot == 3 and has(d):
                        after(pe, "normed", d, 1, 1)
                        after(pe, "maxrows_done", b)
                        for t in range(2):
                            mm = pe.matmul(ps_n[:, 128 * t:128 * t + 128], attn[:, 128 * t:128 * t + 128], wo_in[:, :],
                                           start=(t == 0), stop=True, skip_group_check=True)
                        mm.then_inc(s_["y_ready"], 1)
                    if slot == 6 and has(d):
                        after(pe, "x1_done", d, 2, 2)
                        for t in range(2):
                            mm = pe.transpose(ps_n[:, 128 * t:128 * t + 128], x1[:, t, :], C("ident"))
                        mm.then_inc(s_["x1t_ready"], 1)
                    if slot == 6 and has(b):
                        if has(a):
                            after(pe, "roped", a, 1, 1)
                        for t in range(2):
                            tok = slice(128 * t, 128 * t + 128)
                            mm = three(ps_m[:, 0, tok], (xt_hi[p][:, tok], xt_lo[p][:, tok]),
                                       (w_hi[:, 4, :], w_lo[:, 4, :]), t == 0, t == 1)
                        mm.then_inc(s_["v_ready"], 1)
                    if slot == 8 and has(d):
                        after(pe, "x1l_done", d, 1, 1)
                        for t in range(2):
                            for i, xa in enumerate((x1t_hi, x1t_lo)):
                                mm = pe.matmul(ps_log[:, t], xa[:, 128 * t:128 * t + 128], wg_parts[:, :, :],
                                               start=(t == 0 and i == 0), stop=(i == 1), skip_group_check=True)
                        mm.then_inc(s_["logits_ready"], 1)
                    if slot == 10 and has(d):
                        after(pe, "chosen_done", d, 1, 1)
                        after(pe, "seen_done", d, 2)
                        for t in range(2):
                            terms = [(before_bf, chosen[:, t, :]), (ones_bf, seen[:, :])] + [(ones_bf, chosen[:, 0, :])] * t
                            for i, (l, r) in enumerate(terms):
                                pe.matmul(ps_loc[:, t, :], l[:, :], r, start=(t == 0 and i == 0), stop=(i == len(terms) - 1),
                                          skip_group_check=True)
                        for t in range(2):
                            mm = pe.transpose(ps_route[:, 128 * t:128 * t + 128], chosen_f[:, t, :], C("ident"))
                        mm.then_inc(s_["loc_ready"], 1)
                    if slot == 12 and has(b):
                        after(pe, "parted", b, 2, 2)
                        if has(d):
                            after(pe, "route_done", d, 1, 1)
                        for i in range(NBLK // 4):
                            mm = pe.matmul(ps_n[:, BLK * i:BLK * i + BLK],
                                           max_parts[:, 4 * i:4 * i + 4, :].rearrange("p i m -> p (i m)"), stacked_r[:, :],
                                           start=(i == 0), stop=True, skip_group_check=True)
                        mm.then_inc(s_["ex_ready"], 1)
                    if slot in (11, 13) and has(d):
                        t = (slot - 11) // 2
                        if t == 0:
                            if has(b):
                                after(pe, "vrows_done", b, 1, 1)
                        else:
                            after(pe, "moe_taken", d, 2, 1)
                        for h in range(2):
                            o = ps_m[:, h, :].rearrange("p (e f) -> p e f", e=4)
                            tok = slice(128 * t, 128 * t + 128)
                            three(o, (x1t_hi[:, tok], x1t_lo[:, tok]), (we_hi[:, 4 * h:4 * h + 4, :], we_lo[:, 4 * h:4 * h + 4, :]),
                                  True, False)
                            if h == 0:
                                after(pe, "route_done", d, 1, 1)
                            mm = pe.matmul(ps_m[:, h, :], route[:, tok], route_rows[:, 512 * h:512 * h + 512],
                                           start=False, stop=True, skip_group_check=True)
                        mm.then_inc(s_["moe_ready"], 1)

            all_steps(pe, step)


def constants():
    c = np.zeros((128, NCONST), np.float32)
    def put(name, v, rows=slice(0, 128)):
        at, w = CONSTS[name]
        c[rows, at:at + w] = v
    p = np.arange(128)
    put("ident", np.eye(128))
    put("before", (p[:, None] < p[None, :]))
    inv_freq = (np.float32(1) / np.float32(10000) ** (np.arange(0, HD, 2, dtype=np.float32) / np.float32(HD))).astype(np.float32)
    freqs = (np.arange(S, dtype=np.float32)[None, :] * inv_freq[:, None]).astype(np.float32)
    rows = (p % HD) // 2
    put("cos", np.cos(freqs[rows].astype(np.float64)))
    put("sin", np.sin(freqs[rows].astype(np.float64)))
    r, col = p % BLK, np.arange(BLK)
    put("mask_a", np.where(col[None, :] > r[:, None], NEG, 0.0))
    put("mask_b", np.where(col[None, :] < r[:, None], NEG, 0.0))
    put("stacked", r[:, None] == col[None, :])
    put("head_cols", (p[:, None] // BLK) == ((p[None, :] // HD) % GH))
    put("head_is", (p[:, None] // BLK) == np.arange(GH)[None, :])
    put("tie", (E - np.arange(E))[None, :])
    put("max_sel", -((np.arange(32)[:, None] % H) == np.arange(H)[None, :]).astype(np.float32), slice(SCORE_ROWS, 128))
    sel = np.repeat(np.eye(E, dtype=np.float32), 128, axis=1)
    return c, sel


_INS = ['L0_attn_x', 'L0_attn_wq', 'L0_attn_bq', 'L0_attn_wk', 'L0_attn_bk', 'L0_attn_wv', 'L0_attn_bv', 'L0_attn_wo',
        'L0_attn_bo', 'L0_ffn_wg', 'L0_ffn_W', 'L0_ffn_b']


def kernel(**inputs):
    import numpy as _np
    import concourse.bacc as _bacc
    from concourse import mybir as _mybir
    from concourse.bass_utils import run_bass_kernel_spmd as _run

    nc = _bacc.Bacc("TRN2", target_bir_lowering=False, num_devices=1)
    arrays, args = {}, []
    for name in _INS:
        arrays[f"in_{name}_dram"] = _np.ascontiguousarray(inputs[name])
    table, sel = constants()
    arrays["in_table_dram"] = table
    arrays["in_expert_rows_dram"] = sel
    for name, a in arrays.items():
        args.append(nc.dram_tensor(name, a.shape, _mybir.dt.from_np(a.dtype), kind="ExternalInput").ap())
    args.append(nc.dram_tensor("out_0_dram", (B, S, D), _mybir.dt.float32, kind="ExternalOutput").ap())
    layer_kernel(nc, *args)
    r = _run(nc, [arrays], core_ids=[0])
    return r.results[0]["out_0_dram"]
```

```python
import numpy as np
import concourse.bass as bass
from concourse import mybir
from contextlib import ExitStack

B, S, D = 16, 256, 128
H, HD = 16, 8
E = 8
TOK_TILES = S // 128
CAPACITY = B * S // E
GROUPS, GH = 4, 4
BLK = 32
NBLK = S // BLK
SCORE_ROWS = GH * 3 * HD
EPS = 1e-5
NEG = -3.0e9
BIG = float(2.0 ** 100)
SCALE = float(1.0 / np.sqrt(np.float32(HD)))
V_PITCH, V_ROW = 160, 640
ONES_AT = [64, 224, 256, 416]

CHUNKS = [((j,), (2 * h, 2 * h + 1)) for j in range(4) for h in range(2)]
CHUNKS += [((4,), (0, 1, 2, 3)), ((5, 7), (0, 1, 2, 3)), ((6,), (0, 1, 2, 3))]
NCH = len(CHUNKS)
B_SLOT, PV_SLOT, SLOTS = 2, 3, NCH + 3
EARLY = 2

CONSTS = {}
def _layout():
    at = 0
    for name, w in (("ident", 128), ("before", 128), ("cos", S), ("sin", S), ("mask_a", BLK), ("mask_b", BLK),
                    ("stacked", BLK), ("head_cols", 128), ("head_is", GH), ("tie", E), ("max_sel", H)):
        CONSTS[name] = (at, w)
        at += w
    return at
NCONST = _layout()


def width(j):
    return S - BLK * j


def group_columns(chunk):
    return sum(width(j) for j in chunk[0])


def columns_of(chunk):
    return group_columns(chunk) * len(chunk[1])


def parts_of(chunk):
    blocks, groups = chunk
    return [(j, g, group_columns(chunk) * i + sum(width(b) for b in blocks[:n]))
            for i, g in enumerate(groups) for n, j in enumerate(blocks)]


def layer_kernel(nc, x, wq, bq, wk, bk, wv, bv, wo, bo, wg, W, b, const, expert_rows, out):
    f32, fr, bf = mybir.dt.float32, mybir.dt.float32r, mybir.dt.bfloat16
    ALU, ACT, AX = mybir.AluOpType, mybir.ActivationFunctionType, mybir.AxisListType
    x_t = x.rearrange("b (n p) d -> b p n d", p=128)
    out_t = out.rearrange("b (n p) d -> b p n d", p=128)
    shape = [B, 2, GROUPS, GH, 3, HD, S]
    plain = nc.dram_tensor("plain_parts", shape, f32, kind="Internal").ap()
    turned = nc.dram_tensor("turned_parts", shape, f32, kind="Internal").ap()

    with ExitStack() as ctx:
        def sb(name, shape, dt=f32):
            return ctx.enter_context(nc.sbuf_tensor(name, shape, dt))

        def pb(name, shape):
            return ctx.enter_context(nc.psum_tensor(name, shape, f32))

        def sem(name):
            return ctx.enter_context(nc.semaphore(name))

        cst = sb("cst", [128, NCONST])
        def C(name, rows=slice(0, 128)):
            at, w = CONSTS[name]
            return cst[rows, at:at + w]

        w_in = sb("w_in", [128, 5, 128])
        w_hi, w_lo = sb("w_hi", [128, 5, 128], fr), sb("w_lo", [128, 5, 128], fr)
        bias_rows = sb("bias_rows", [1, 6, 128])
        bias_cols = sb("bias_cols", [128, 5])
        bv_wide = sb("bv_wide", [128, 128])
        wo_in = sb("wo_in", [128, 128])
        out_bias = sb("out_bias", [128, 128])
        PR = 3
        probs = sb("probs", [128, PR, 512])
        w_exp = probs[:, 0:2, :].rearrange("p a (e f) -> p (a e) f", f=128)
        we_hi, we_lo = sb("we_hi", [128, E, 128], fr), sb("we_lo", [128, E, 128], fr)
        wg_in = sb("wg_in", [128, E])
        wg_parts = sb("wg_parts", [128, 2, E], fr)
        rot_cs = sb("rot_cs", [128, 2, 2, S])
        rot_c, rot_s = rot_cs[:, 0], rot_cs[:, 1]
        rows_in = sb("rows_in", [E, E * 128])
        b_row = sb("b_row", [1, E * 128])
        route_rows = sb("route_rows", [128, E * 128], fr)
        ident_bf = sb("ident_bf", [128, 128], bf)
        mask_a_bf, mask_b_bf = sb("mask_a_bf", [128, BLK], bf), sb("mask_b_bf", [128, BLK], bf)
        stacked_r = sb("stacked_r", [128, BLK], fr)
        before_bf, ones_bf = sb("before_bf", [128, 128], bf), sb("ones_bf", [128, 128], bf)
        zero = sb("zero", [128, 1])
        one, minus_half = sb("one", [1, 128]), sb("minus_half", [128, 2])

        x_in = sb("x_in", [128, 2, 128])
        xt_hi = [sb(f"xt_hi{p}", [128, S], fr) for p in range(2)]
        xt_lo = [sb(f"xt_lo{p}", [128, S], fr) for p in range(2)]
        rot = sb("rot", [128, 2, S])
        rot_hi, rot_lo = sb("rot_hi", [128, 2, S], fr), sb("rot_lo", [128, 2, S], fr)
        turn_hi, turn_lo = sb("turn_hi", [128, 2, S], fr), sb("turn_lo", [128, 2, S], fr)
        v_rows = sb("v_rows", [128, 2, 128])
        q_diag = [sb(f"q_diag{p}", [128, GROUPS, GH, S], fr) for p in range(2)]
        k_plain = [sb(f"k_plain{p}", [128, GROUPS, S], fr) for p in range(2)]
        row_max = sb("row_max", [128, NBLK, GROUPS])
        max_wide = sb("max_wide", [128, NBLK, H])
        max_parts = sb("max_parts", [128, NBLK, 2 * H], fr)
        max_rows = sb("max_rows", [32, S], fr)
        v_diag = [sb(f"v_diag{p}", [128, NBLK, V_ROW]) for p in range(2)]
        k_diag = [sb(f"k_diag{p}", [128, GROUPS, GH, S], fr) for p in range(2)]
        q_plain = [sb(f"q_plain{p}", [128, GROUPS, S], fr) for p in range(2)]
        weighted, sums = sb("weighted", [128, S]), sb("sums", [128, S])
        inv_den = sb("inv_den", [128, S])
        attn = sb("attn", [128, S])
        x_res, x_bias = sb("x_res", [128, 2, 128]), sb("x_bias", [128, 2, 128])
        z1, x1, z2 = sb("z1", [128, 2, 128]), sb("x1", [128, 2, 128]), sb("z2", [128, 2, 128])
        y_sel, y_out = sb("y_sel", [128, 2, 128]), sb("y_out", [128, 2, 128])
        st1, mv1, rs1 = sb("st1", [128, 2, 6]), sb("mv1", [128, 2, 2]), sb("rs1", [128, 2])
        st2, mv2, rs2 = sb("st2", [128, 2, 6]), sb("mv2", [128, 2, 2]), sb("rs2", [128, 2])
        x1t_hi, x1t_lo = sb("x1t_hi", [128, S], fr), sb("x1t_lo", [128, S], fr)
        logits = sb("logits", [128, 2, E])
        top, below, e_gate = sb("top", [128, 2]), sb("below", [128, 2, E]), sb("e_gate", [128, 2, E])
        e_sum, gate = sb("e_sum", [128, 2]), sb("gate", [128, 2])
        rank, first = sb("rank", [128, 2, E]), sb("first", [128, 2])
        chosen, chosen_f = sb("chosen", [128, 2, E], bf), sb("chosen_f", [128, 2, E])
        seen = sb("seen", [128, E], bf)
        kept, n_kept, gate_kept = sb("kept", [128, 2, E]), sb("n_kept", [128, 2]), sb("gate_kept", [128, 2])
        route = sb("route", [128, S], fr)

        ps_a = [pb(f"ps_a{i}", [128, 512]) for i in range(2)]
        ps_b = [pb(f"ps_b{i}", [128, 512]) for i in range(2)]
        ps_pv = pb("ps_pv", [128, 2, S])
        ps_m = pb("ps_m", [128, 2, 512])
        ps_n = pb("ps_n", [128, 512])
        ps_log = ps_n[:, 0:4 * E].rearrange("p (t w e) -> p t w e", t=2, w=2)
        ps_loc = ps_n[:, 32:32 + 2 * E].rearrange("p (t e) -> p t e", t=2)
        ps_route = ps_n[0:E, 64:64 + S]

        names = []
        names += """w_loaded late_loaded tables_loaded x_loaded res_loaded a_parts_written b_parts_written
                    aops_loaded0 aops_loaded1 bops_loaded0 bops_loaded1 maxrows_loaded stored""".split()
        names += """start_dve start_pool start_act swapped w_split bias_ps bias_done late_dve late_pe""".split()
        names += """xt_ready xh_done xl_done qk_ready roped rot_done""".split()
        names += """rothi_done rotlo_done turnhi_done turnlo_done""".split()
        names += """a_ready a_taken widened parted ex_ready maxrows_done v_ready vrows_done v_done""".split()
        names += """b_ready exp_done pv_ready""".split()
        names += """pv_copied sums_copied den_done normed xb_done y_ready z1_done st1_done mv1_done ve1_done
                    rs1_done x1_done""".split()
        names += """x1t_ready x1h_done x1l_done logits_ready logits_done top_done below_done egate_done gate_sum
                    gate_done rank_done first_done chosen_done seen_done loc_ready route_done nkept_done gk_done
                    moe_ready moe_taken""".split()
        names += """z2_done st2_done mv2_done ve2_done rs2_done out_done""".split()
        s_ = {name: sem(name) for name in names}

        def after(eng, name, t, per=1, k=0):
            n = t * per + k
            if isinstance(n, int):
                n = min(n, B * per)
                if n <= 0:
                    return
            eng.wait_ge(s_[name], n)

        def parts_free(eng, a):
            after(eng, "a_parts_written", a, PARTS_WRITTEN)
            after(eng, "b_parts_written", a, PARTS_WRITTEN)

        def of_seq(v, t):
            return v[t] if isinstance(t, int) else v[bass.ds(t, 1)].squeeze(0)

        def diag_block(t, g, j):
            return t[:, g, :, :].rearrange("p h x -> p (h x)")[:, j:GH * S:NBLK]

        def is_step(s, which):
            return isinstance(s, int) and s == which

        def has(t):
            return not isinstance(t, int) or 0 <= t < B

        def maxima_at(slot, a, b):
            if slot < NCH - EARLY:
                return (b, slot + EARLY) if has(b) else (None, 0)
            if slot >= SLOTS - EARLY:
                return (a, slot - (SLOTS - EARLY)) if has(a) else (None, 0)
            return None, 0

        block = ctx.enter_context(nc.Block())

        def all_steps(eng, step):
            for s in range(-2, 3):
                step(s, s % 2, lambda o: (s + o) // 2)
            with eng.Fori(0, (B - 6) // 2) as u:
                for k in range(2):
                    step(u * 2 + (3 + k), (3 + k) % 2, lambda o: u + (3 + k + o) // 2)
            for s in range(B - 3, B + 2):
                step(s, s % 2, lambda o: (s + o) // 2)

        W_LOADED, LATE_LOADED = 7 * 16, 5 * 16
        PARTS_WRITTEN, OPS_LOADED = 6 * 16, (1 + GH) * 16
        Q_HI, Q_LO, K_HI, K_LO = (0, 1), (2,), (1, 2), (0,)

        @block.sync
        def _(sp):
            sp.dma_start(cst[:, :], const).then_inc(s_["tables_loaded"], 16)
            sp.dma_start(x_in[:, :, :], of_seq(x_t, 0)).then_inc(s_["x_loaded"], 16)
            w = s_["w_loaded"]
            for i, a in ((0, wq), (2, wk), (4, wv)):
                sp.dma_start(w_in[:, i, :], a).then_inc(w, 16)
            for i, a in ((0, bq), (2, bk), (4, bv), (5, bo)):
                sp.dma_start(bias_rows[:, i, :], a.rearrange("(o n) -> o n", o=1)).then_inc(w, 16)
            w = s_["late_loaded"]
            sp.dma_start(w_exp[:, :, :], W.rearrange("e f h -> f e h")).then_inc(w, 16)
            sp.dma_start(wo_in[:, :], wo).then_inc(w, 16)
            sp.dma_start(wg_in[:, :], wg).then_inc(w, 16)
            sp.dma_start(b_row[:, :], b.rearrange("(o e) f -> o (e f)", o=1)).then_inc(w, 16)
            sp.dma_start(rows_in[:, :], expert_rows).then_inc(w, 16)

            def step(s, p, half):
                n, a, b, c, d, e = s + 2, s + 1, s, s - 1, s - 2, s - 3
                q = 1 - p
                if has(n) and not is_step(s, -2):
                    after(sp, "xt_ready", n)
                    sp.dma_start(x_in[:, :, :], of_seq(x_t, n)).then_inc(s_["x_loaded"], 16)
                if has(d):
                    after(sp, "xb_done", d)
                    sp.dma_start(x_res[:, :, :], of_seq(x_t, d)).then_inc(s_["res_loaded"], 16)
                if has(a):
                    def write(src, dst, qk, taus, name, done):
                        after(sp, done, a, 1, 1)
                        sp.nop(nofuse=True)
                        for tau in taus:
                            sp.dma_start(of_seq(dst, a)[qk, :, :, tau].rearrange("g h d x -> (g h) d x"),
                                         src[:, qk, :].bitcast(f32)).then_inc(s_[name], 16)
                    write(rot_hi, plain, 1, K_HI, "a_parts_written", "rothi_done")
                    write(turn_hi, turned, 0, Q_HI, "a_parts_written", "turnhi_done")
                    write(rot_lo, plain, 1, K_LO, "a_parts_written", "rotlo_done")
                    write(turn_lo, turned, 0, Q_LO, "a_parts_written", "turnlo_done")
                    write(rot_hi, plain, 0, Q_HI, "b_parts_written", "rothi_done")
                    write(rot_lo, plain, 0, Q_LO, "b_parts_written", "rotlo_done")
                    after(sp, "a_parts_written", a, PARTS_WRITTEN, PARTS_WRITTEN)
                    sp.nop(nofuse=True)
                    qp, kp = of_seq(turned, a)[0], of_seq(plain, a)[1]
                    if is_step(s, -1) or is_step(s, 0):
                        sp.wait_ge(s_["start_pool"], 1 + 2 * a)
                    after(sp, "a_ready", a - 2, NCH, NCH)
                    sp.dma_start(k_plain[q][0:SCORE_ROWS, :, :].bitcast(f32), kp.rearrange("g h t d x -> (h t d) g x"))\
                        .then_inc(s_[f"aops_loaded{q}"], 16)
                    for hl in range(GH):
                        sp.dma_start(q_diag[q][24 * hl:24 * hl + 24, :, hl, :].bitcast(f32),
                                     qp[:, hl].rearrange("g t d x -> (t d) g x")).then_inc(s_[f"aops_loaded{q}"], 16)
                    write(turn_hi, turned, 1, K_HI, "b_parts_written", "turnhi_done")
                    write(turn_lo, turned, 1, K_LO, "b_parts_written", "turnlo_done")
                if has(b):
                    if is_step(s, 0) or is_step(s, 1):
                        sp.wait_ge(s_["start_pool"], 2 + 2 * b)
                    after(sp, "pv_ready", b - 2, NCH, NCH)
                    after(sp, "b_parts_written", b, PARTS_WRITTEN, PARTS_WRITTEN)
                    sp.nop(nofuse=True)
                    kp, qp = of_seq(turned, b)[1], of_seq(plain, b)[0]
                    sp.dma_start(q_plain[p][0:SCORE_ROWS, :, :].bitcast(f32), qp.rearrange("g h t d x -> (h t d) g x"))\
                        .then_inc(s_[f"bops_loaded{p}"], 16)
                    for hl in range(GH):
                        sp.dma_start(k_diag[p][24 * hl:24 * hl + 24, :, hl, :].bitcast(f32),
                                     kp[:, hl].rearrange("g t d x -> (t d) g x")).then_inc(s_[f"bops_loaded{p}"], 16)

            all_steps(sp, step)

        @block.gpsimd
        def _(pool):
            def inverse_deviation(mv, rs, n, d):
                after(pool, f"mv{n}_done", d, 2, 2)
                pool.nop(nofuse=True)
                pool.tensor_scalar(rs[:, :], mv[:, :, 1], EPS, None, ALU.add).then_inc(s_[f"ve{n}_done"], 1)
                after(pool, f"ve{n}_done", d, 1, 1)
                pool.tensor_tensor(rs[:, :], rs[:, :], minus_half[:, :], ALU.pow).then_inc(s_[f"rs{n}_done"], 1)

            def output(e):
                inverse_deviation(mv2, rs2, 2, e)
                after(pool, "rs2_done", e, 1, 1)
                after(pool, "stored", e, 16)
                pool.nop(nofuse=True)
                for t in range(2):
                    last = pool.tensor_scalar(y_out[:, t, :], z2[:, t, :], mv2[:, t, 0:1], rs2[:, t:t + 1],
                                              ALU.subtract, ALU.mult)
                last.then_inc(s_["out_done"], 1)
                after(pool, "out_done", e, 1, 1)
                pool.nop(nofuse=True)
                pool.dma_start(of_seq(out_t, e), y_out[:, :, :]).then_inc(s_["stored"], 16)

            pool.memset(minus_half[:, :], -0.5)
            pool.memset(q_diag[0][:, :, :, :].bitcast(f32), 0.0)
            pool.memset(k_plain[0][:, :, :].bitcast(f32), 0.0).then_inc(s_["start_pool"], 1)
            pool.memset(route_rows[:, :].bitcast(f32), 0.0)
            pool.memset(k_diag[0][:, :, :, :].bitcast(f32), 0.0)
            pool.memset(q_plain[0][:, :, :].bitcast(f32), 0.0).then_inc(s_["start_pool"], 1)

            def start_late():
                pool.memset(q_diag[1][:, :, :, :].bitcast(f32), 0.0)
                pool.memset(k_plain[1][:, :, :].bitcast(f32), 0.0).then_inc(s_["start_pool"], 1)
                pool.memset(seen[:, :], 0.0)
                pool.memset(k_diag[1][:, :, :, :].bitcast(f32), 0.0)
                pool.memset(q_plain[1][:, :, :].bitcast(f32), 0.0).then_inc(s_["start_pool"], 1)

            def step(s, p, half):
                n, a, b, c, d, e = s + 2, s + 1, s, s - 1, s - 2, s - 3
                if has(a):
                    after(pool, "rothi_done", a, 1, 1)
                    parts_free(pool, a)
                    pool.tensor_tensor(rot_lo[:, :, :], rot[:, :, :], rot_hi[:, :, :].bitcast(f32), ALU.subtract)\
                        .then_inc(s_["rotlo_done"], 1)
                if has(d):
                    after(pool, "res_loaded", d, 16, 16)
                    after(pool, "z1_done", d)
                    if is_step(s, 2):
                        pool.wait_ge(s_["late_dve"], 4)
                    pool.tensor_tensor(x_bias[:, :, :], x_res[:, :, :],
                                       out_bias[:, :].unsqueeze(1).broadcast_to([128, 2, 128]), ALU.add)\
                        .then_inc(s_["xb_done"], 1)
                    inverse_deviation(mv1, rs1, 1, d)
                if is_step(s, -1):
                    start_late()
                if has(b):
                    after(pool, "vrows_done", b, 1, 1)
                    after(pool, "pv_ready", b - 2, NCH, NCH)
                    if has(d):
                        after(pool, "rs1_done", d, 1, 1)
                    if has(a):
                        after(pool, "rotlo_done", a, 1, 1)
                    pool.nop(nofuse=True)
                    for jj in range(4):
                        for hl in range(GH):
                            dst = v_diag[p][BLK * hl:BLK * hl + BLK, jj:NBLK:4, :].rearrange("p t (g c) -> p t g c", c=V_PITCH)
                            src = v_rows[BLK * jj:BLK * jj + BLK, :, :].rearrange("p t (g c) -> p t g c", g=GROUPS)
                            last = pool.tensor_copy(dst[:, :, :, HD * hl:HD * hl + HD], src[:, :, :, HD * hl:HD * hl + HD])
                    last.then_inc(s_["v_done"], 1)
                    after(pool, "v_done", b, 1, 1)
                if has(d):
                    after(pool, "loc_ready", d, 1, 1)
                    for t in range(TOK_TILES):
                        pool.tensor_tensor(seen[:, :], seen[:, :], chosen[:, t, :], ALU.add).then_inc(s_["seen_done"], 1)
                        after(pool, "seen_done", d, 2, t + 1)
                if has(e):
                    output(e)

            all_steps(pool, step)
            output(B - 1)
            pool.wait_ge(s_["stored"], 16 * B)

        @block.scalar
        def _(act):
            def mark_heads(p):
                act.wait_ge(s_["tables_loaded"], 16)
                act.wait_ge(s_["start_pool"], 2 + 2 * p)
                for g in range(GROUPS):
                    last = act.activation(
                        k_diag[p][SCORE_ROWS:128, g, :, :],
                        C("max_sel", slice(SCORE_ROWS, 128))[:, GH * g:GH * g + GH].unsqueeze(2).broadcast_to([32, GH, S]),
                        ACT.Copy)
                last.then_inc(s_["start_act"], 1)

            def copy_pairs(to, at):
                act.activation(to[0:64, :], ps_pv[64 * at:64 * at + 64, 0, :], ACT.Copy)
                return act.activation(to[64:128, :], ps_pv[64 - 64 * at:128 - 64 * at, 1, :], ACT.Copy)

            act.wait_ge(s_["start_dve"], 1)
            act.activation(v_diag[1][:, :, 0:512], zero[:, :].unsqueeze(2).broadcast_to([128, NBLK, 512]), ACT.Copy)\
                .then_inc(s_["start_act"], 1)

            def step(s, p, half):
                n, a, b, c, d = s + 2, s + 1, s, s - 1, s - 2
                for slot in range(SLOTS):
                    k = slot - B_SLOT
                    if has(c) and 0 <= k < NCH:
                        cols = columns_of(CHUNKS[k])
                        after(act, "b_ready", c, NCH, k + 1)
                        after(act, "pv_ready", c, NCH, k + 1 - PR)
                        act.activation(probs[:, k % PR, 0:cols], ps_b[k % 2][:, 0:cols], ACT.Exp, scale=SCALE)\
                            .then_inc(s_["exp_done"], 1)
                    if slot == 0 and has(d):
                        copy_pairs(weighted, 0).then_inc(s_["pv_copied"], 1)
                    if slot == 7 and has(d):
                        after(act, "x1t_ready", d, 1, 1)
                        act.activation(x1t_hi[:, :], ps_n[:, 0:S], ACT.Copy).then_inc(s_["x1h_done"], 1)
                    if slot == 7 and has(n):
                        after(act, "xt_ready", n, 1, 1)
                        after(act, "v_ready", n - 2, 1, 1)
                        act.activation(xt_hi[p][:, :], ps_m[:, 1, 0:S], ACT.Copy).then_inc(s_["xh_done"], 1)
                    if slot == 8 and has(b):
                        after(act, "v_ready", b, 1, 1)
                        after(act, "v_done", b)
                        act.activation(v_rows[:, :, :], ps_m[:, 0, 0:256].rearrange("p (t c) -> p t c", t=2), ACT.Copy)\
                            .then_inc(s_["vrows_done"], 1)
                    if slot == 4 and has(a):
                        after(act, "rot_done", a, 1, 1)
                        parts_free(act, a)
                        act.activation(rot_hi[:, :, :], rot[:, :, :], ACT.Copy).then_inc(s_["rothi_done"], 1)
                        act.activation(turn_hi[:, :, :].rearrange("p i (r j) -> p i j r", j=NBLK),
                                       rot[:, :, :].rearrange("p i (j r) -> p i j r", j=NBLK), ACT.Copy)\
                            .then_inc(s_["turnhi_done"], 1)
                    if slot == 5 and has(a):
                        after(act, "rotlo_done", a, 1, 1)
                        act.activation(turn_lo[:, :, :].rearrange("p i (r j) -> p i j r", j=NBLK),
                                       rot_lo[:, :, :].bitcast(f32).rearrange("p i (j r) -> p i j r", j=NBLK), ACT.Copy)\
                            .then_inc(s_["turnlo_done"], 1)
                    if slot == 6 and (is_step(s, -1) or is_step(s, 0)):
                        mark_heads(a)
                    if slot == 11 and has(b):
                        after(act, "ex_ready", b, 1, 1)
                        after(act, "maxrows_loaded", b, 16)
                        for i in range(4):
                            last = act.activation(max_rows[:, :].rearrange("m (i2 i r) -> m i i2 r", i2=2, i=4)[:, i],
                                                  ps_n[32 * i:32 * i + 32, 0:2 * BLK].rearrange("m (i2 r) -> m i2 r", i2=2),
                                                  ACT.Copy)
                        last.then_inc(s_["maxrows_done"], 1)
                        after(act, "maxrows_done", b, 1, 1)
                        after(act, "pv_ready", b - 2, NCH, NCH)
                        act.dma_start(q_plain[p][SCORE_ROWS:128, :, :].bitcast(f32),
                                      max_rows[:, :].bitcast(f32).unsqueeze(1).broadcast_to([32, GROUPS, S]))\
                            .then_inc(s_["maxrows_loaded"], 16)
                    if slot == 13 and has(c):
                        after(act, "pv_ready", c, NCH, NCH)
                        after(act, "normed", c)
                        copy_pairs(sums, 1).then_inc(s_["sums_copied"], 1)
                    if slot == 10 and has(d):
                        after(act, "below_done", d, 1, 1)
                        act.activation(e_gate[:, :, :], below[:, :, :], ACT.Exp).then_inc(s_["egate_done"], 1)
            all_steps(act, step)

        @block.vector
        def _(dve):
            dve.memset(zero[:, :], 0.0).then_inc(s_["start_dve"], 1)
            dve.memset(one[:, :], 1.0)
            dve.memset(v_diag[0][:, :, 0:512], 0.0).then_inc(s_["start_dve"], 1)
            dve.wait_ge(s_["w_loaded"], W_LOADED)
            for i in (0, 2):
                for t, rows in ((w_in, 128), (bias_rows, 1)):
                    src, dst = (t[0:rows, i + o, :].rearrange("p (m two) -> p m two", two=2) for o in (0, 1))
                    dve.tensor_scalar(dst[:, :, 0], src[:, :, 1], -1.0, None, ALU.mult)
                    last = dve.tensor_copy(dst[:, :, 1], src[:, :, 0])
            last.then_inc(s_["swapped"], 1)
            dve.wait_ge(s_["swapped"], 1)
            dve.tensor_copy(w_hi[:, :, :], w_in[:, :, :]).then_inc(s_["w_split"], 1)
            dve.wait_ge(s_["w_split"], 1)
            dve.tensor_tensor(w_lo[:, :, :], w_in[:, :, :], w_hi[:, :, :].bitcast(f32), ALU.subtract)\
                .then_inc(s_["w_split"], 1)
            dve.wait_ge(s_["bias_ps"], 1)
            dve.tensor_copy(bias_cols[:, :], ps_n[:, 0:5]).then_inc(s_["bias_done"], 1)
            dve.wait_ge(s_["bias_done"], 1)

            def start_late():
                dve.tensor_copy(bv_wide[:, :], bias_cols[:, 4:5].broadcast_to([128, 128])).then_inc(s_["late_dve"], 1)
                dve.wait_ge(s_["late_pe"], 1)
                turned_w = ps_m[:, :, :].rearrange("p a (e f) -> p (a e) f", e=4)
                dve.tensor_copy(we_hi[:, :, :], turned_w).then_inc(s_["late_dve"], 1)
                dve.wait_ge(s_["late_dve"], 2)
                dve.tensor_tensor(we_lo[:, :, :], turned_w, we_hi[:, :, :].bitcast(f32), ALU.subtract)\
                    .then_inc(s_["late_dve"], 1)
                dve.wait_ge(s_["late_pe"], 2)
                dve.tensor_copy(out_bias[:, :], ps_n[:, 0:128]).then_inc(s_["late_dve"], 1)
                dve.tensor_copy(ident_bf[:, :], C("ident"))
                dve.tensor_copy(mask_a_bf[:, :], C("mask_a"))
                dve.tensor_copy(mask_b_bf[:, :], C("mask_b"))
                dve.tensor_copy(stacked_r[:, :], C("stacked"))
                dve.tensor_copy(before_bf[:, :], C("before"))
                dve.memset(ones_bf[:, :], 1.0)
                dve.memset(route[:, :].bitcast(f32), 1.0)
                dve.wait_ge(s_["late_loaded"], LATE_LOADED)
                dve.tensor_copy(wg_parts[:, 0, :], wg_in[:, :])
                dve.wait_ge(s_["start_pool"], 2)
                dve.tensor_copy(route_rows[0:E, :], rows_in[:, :])
                dve.tensor_copy(route_rows[32:33, :], b_row[:, :]).then_inc(s_["late_dve"], 1)
                dve.wait_ge(s_["late_dve"], 5)
                dve.tensor_tensor(route_rows[64:65, :], b_row[:, :], route_rows[32:33, :].bitcast(f32), ALU.subtract)
                dve.tensor_tensor(wg_parts[:, 1, :], wg_in[:, :], wg_parts[:, 0, :].bitcast(f32), ALU.subtract)\
                    .then_inc(s_["late_dve"], 1)
                dve.wait_ge(s_["start_dve"], 2)
                dve.wait_ge(s_["start_act"], 1)
                for p in range(2):
                    for g in range(GROUPS):
                        last = dve.tensor_copy(v_diag[p][:, :, ONES_AT[g]:ONES_AT[g] + 32],
                                               C("head_cols")[:, 0:32].unsqueeze(1).broadcast_to([128, NBLK, 32]))
                last.then_inc(s_["late_dve"], 1)

            def norm_stats(z, st, mv, n, d):
                after(dve, f"z{n}_done", d, 1, 1)
                for t in range(2):
                    dve.bn_stats(st[:, t, :], z[:, t, :]).then_inc(s_[f"st{n}_done"], 1)
                for t in range(2):
                    after(dve, f"st{n}_done", d, 2, t + 1)
                    dve.nop(nofuse=True)
                    dve.bn_aggr(mv[:, t, :], st[:, t, :]).then_inc(s_[f"mv{n}_done"], 1)

            def add_experts(e):
                after(dve, "out_done", e)
                for t in range(2):
                    after(dve, "moe_taken", e, 2, t + 1)
                    after(dve, "gk_done", e, 1, 1)
                    last = dve.scalar_tensor_tensor(out=z2[:, t, :], in0=y_sel[:, t, :], scalar=gate_kept[:, t:t + 1],
                                                    in1=x1[:, t, :], op0=ALU.mult, op1=ALU.add)
                last.then_inc(s_["z2_done"], 1)

            def select(d, t):
                after(dve, "moe_ready", d, 2, t + 1)
                dve.tensor_reduce(y_sel[:, t, :], ps_m[:, :, :].rearrange("p a (e f) -> p f (a e)", e=4),
                                  AX.X, ALU.max).then_inc(s_["moe_taken"], 1)

            def step(s, p, half):
                n, a, b, c, d, e = s + 2, s + 1, s, s - 1, s - 2, s - 3
                for slot in range(SLOTS):
                    t, k = maxima_at(slot, a, b)
                    if t is not None:
                        after(dve, "a_ready", t, NCH, k + 1)
                        if k == 0:
                            after(dve, "widened", t)
                        blocks, groups = CHUNKS[k]
                        scores = ps_a[k % 2][:, 0:columns_of(CHUNKS[k])].rearrange("p (g x) -> p g x", g=len(groups))
                        col = 0
                        for j in blocks:
                            last = dve.tensor_reduce(row_max[:, NBLK - 1 - j, groups[0]:groups[-1] + 1],
                                                     scores[:, :, col:col + width(j)], AX.X, ALU.max)
                            col += width(j)
                        last.then_inc(s_["a_taken"], 1)
                    if slot in (12, 13) and has(d):
                        select(d, slot - 12)
                    if slot in (1, 2) and has(d):
                        after(dve, "sums_copied", d, 1, 1)
                        half_cols = slice(128 * (slot - 1), 128 * slot)
                        dve.reciprocal(inv_den[:, half_cols], sums[:, half_cols]).then_inc(s_["den_done"], 1)
                    if slot == 2 and has(d):
                        after(dve, "pv_copied", d, 1, 1)
                        after(dve, "y_ready", d)
                        after(dve, "den_done", d, 2, 2)
                        dve.tensor_tensor(attn[:, :], weighted[:, :], inv_den[:, :], ALU.mult).then_inc(s_["normed"], 1)
                    if slot == 3 and has(e):
                        add_experts(e)
                    if slot == 4 and has(d):
                        after(dve, "y_ready", d, 1, 1)
                        after(dve, "xb_done", d, 1, 1)
                        dve.tensor_tensor(z1[:, :, :], ps_n[:, 0:2 * 128].rearrange("p (t f) -> p t f", t=2),
                                          x_bias[:, :, :], ALU.add).then_inc(s_["z1_done"], 1)
                        norm_stats(z1, st1, mv1, 1, d)
                    if slot == 5 and has(d):
                        after(dve, "rs1_done", d, 1, 1)
                        for t in range(2):
                            dve.tensor_scalar(x1[:, t, :], z1[:, t, :], mv1[:, t, 0:1], rs1[:, t:t + 1],
                                              ALU.subtract, ALU.mult).then_inc(s_["x1_done"], 1)
                    if slot == 11 and has(e):
                        norm_stats(z2, st2, mv2, 2, e)
                    if slot == 7 and has(d):
                        after(dve, "x1h_done", d, 1, 1)
                        dve.tensor_tensor(x1t_lo[:, :], ps_n[:, 0:S], x1t_hi[:, :].bitcast(f32), ALU.subtract)\
                            .then_inc(s_["x1l_done"], 1)
                    if slot == 8 and has(n):
                        after(dve, "xh_done", n, 1, 1)
                        dve.tensor_tensor(xt_lo[p][:, :], ps_m[:, 1, 0:S], xt_hi[p][:, :].bitcast(f32), ALU.subtract)\
                            .then_inc(s_["xl_done"], 1)
                    if slot == 9 and has(b):
                        after(dve, "a_taken", b, NCH, NCH)
                        dve.tensor_tensor(max_wide[:, :, :].rearrange("p i (g h) -> p (i g) h", g=GROUPS),
                                          row_max[:, :, :].rearrange("p i g -> p (i g)").unsqueeze(2)
                                          .broadcast_to([128, NBLK * GROUPS, GH]),
                                          C("head_is").unsqueeze(1).broadcast_to([128, NBLK * GROUPS, GH]), ALU.mult)\
                            .then_inc(s_["widened"], 1)
                        after(dve, "widened", b, 1, 1)
                        dve.tensor_copy(max_parts[:, :, 0:H], max_wide[:, :, :]).then_inc(s_["parted"], 1)
                        after(dve, "parted", b, 2, 1)
                        dve.tensor_tensor(max_parts[:, :, H:2 * H], max_wide[:, :, :], max_parts[:, :, 0:H].bitcast(f32),
                                          ALU.subtract).then_inc(s_["parted"], 1)
                    if slot == 9 and has(d):
                        after(dve, "logits_ready", d, 1, 1)
                        dve.tensor_reduce(logits[:, :, :], ps_log.rearrange("p t w e -> p t e w"), AX.X, ALU.add)\
                            .then_inc(s_["logits_done"], 1)
                        after(dve, "logits_done", d, 1, 1)
                        dve.tensor_reduce(top[:, :], logits[:, :, :], AX.X, ALU.max).then_inc(s_["top_done"], 1)
                        after(dve, "top_done", d, 1, 1)
                        dve.tensor_tensor(below[:, :, :], logits[:, :, :], top[:, :].unsqueeze(2).broadcast_to([128, 2, E]),
                                          ALU.subtract).then_inc(s_["below_done"], 1)
                        after(dve, "below_done", d, 1, 1)
                        dve.scalar_tensor_tensor(out=rank[:, :, :], in0=below[:, :, :], scalar=0.0,
                                                 in1=C("tie").unsqueeze(1).broadcast_to([128, 2, E]),
                                                 op0=ALU.is_ge, op1=ALU.mult).then_inc(s_["rank_done"], 1)
                        after(dve, "rank_done", d, 1, 1)
                        dve.tensor_reduce(first[:, :], rank[:, :, :], AX.X, ALU.max).then_inc(s_["first_done"], 1)
                        after(dve, "first_done", d, 1, 1)
                        after(dve, "seen_done", d, 2)
                        dve.tensor_tensor(chosen[:, :, :], rank[:, :, :], first[:, :].unsqueeze(2).broadcast_to([128, 2, E]),
                                          ALU.is_equal)
                        dve.tensor_tensor(chosen_f[:, :, :], rank[:, :, :], first[:, :].unsqueeze(2).broadcast_to([128, 2, E]),
                                          ALU.is_equal).then_inc(s_["chosen_done"], 1)
                    if slot == 10 and has(d):
                        after(dve, "egate_done", d, 1, 1)
                        dve.tensor_reduce(e_sum[:, :], e_gate[:, :, :], AX.X, ALU.add).then_inc(s_["gate_sum"], 1)
                        after(dve, "gate_sum", d, 1, 1)
                        dve.reciprocal(gate[:, :], e_sum[:, :]).then_inc(s_["gate_done"], 1)
                        after(dve, "loc_ready", d, 1, 1)
                        dve.tensor_scalar(route[0:E, :], ps_route, -1.0, BIG, ALU.add, ALU.mult)
                        dve.scalar_tensor_tensor(out=kept[:, :, :], in0=ps_loc, scalar=float(CAPACITY),
                                                 in1=chosen_f[:, :, :], op0=ALU.is_lt, op1=ALU.mult)\
                            .then_inc(s_["route_done"], 1)
                        after(dve, "route_done", d, 1, 1)
                        dve.tensor_reduce(n_kept[:, :], kept[:, :, :], AX.X, ALU.add).then_inc(s_["nkept_done"], 1)
                        after(dve, "nkept_done", d, 1, 1)
                        dve.tensor_tensor(gate_kept[:, :], n_kept[:, :], gate[:, :], ALU.mult).then_inc(s_["gk_done"], 1)
                    if slot == 10 and has(n):
                        after(dve, "qk_ready", n, 1, 1)
                        for i in range(2):
                            dve.scalar_tensor_tensor(out=rot_c[:, i, :], in0=ps_m[:, 0, S * i:S * i + S],
                                                     scalar=bias_cols[:, 2 * i:2 * i + 1], in1=C("cos"),
                                                     op0=ALU.add, op1=ALU.mult)
                            last = dve.scalar_tensor_tensor(out=rot_s[:, i, :], in0=ps_m[:, 1, S * i:S * i + S],
                                                            scalar=bias_cols[:, 2 * i + 1:2 * i + 2], in1=C("sin"),
                                                            op0=ALU.add, op1=ALU.mult)
                        last.then_inc(s_["roped"], 1)
                        after(dve, "roped", n, 1, 1)
                        after(dve, "rotlo_done", n)
                        after(dve, "turnhi_done", n)
                        dve.tensor_tensor(rot[:, :, :], rot_c[:, :, :], rot_s[:, :, :], ALU.add).then_inc(s_["rot_done"], 1)
                    if slot == 10 and is_step(s, -2):
                        start_late()

            all_steps(dve, step)
            add_experts(B - 1)
            norm_stats(z2, st2, mv2, 2, B - 1)

        @block.tensor
        def _(pe):
            pe.wait_ge(s_["swapped"], 1)
            for i in range(5):
                mm = pe.matmul(ps_n[:, i:i + 1], bias_rows[0:1, i, :], one[0:1, 0:1], start=(i == 0), stop=True,
                               skip_group_check=True)
            mm.then_inc(s_["bias_ps"], 1)
            pe.wait_ge(s_["bias_done"], 1)
            pe.wait_ge(s_["tables_loaded"], 16)

            def start_late():
                pe.wait_ge(s_["late_loaded"], LATE_LOADED)
                pe.wait_ge(s_["roped"], 1)
                for e in range(E):
                    mm = pe.transpose(ps_m[:, e // 4, 128 * (e % 4):128 * (e % 4) + 128], w_exp[:, e, :], C("ident"))
                mm.then_inc(s_["late_pe"], 1)
                pe.wait_ge(s_["late_dve"], 1)
                pe.matmul(ps_n[:, 0:128], bv_wide[:, :], wo_in[:, :], start=True, stop=False)
                pe.matmul(ps_n[:, 0:128], one[0:1, :], bias_rows[0:1, 5, :], start=False, stop=True).then_inc(s_["late_pe"], 1)
                pe.wait_ge(s_["late_dve"], 4)

            def three(out, st, mv, start, stop):
                (sh, sl), (mh, ml) = st, mv
                pe.matmul(out, sh, mh, start=start, stop=False, skip_group_check=True)
                pe.matmul(out, sh, ml, start=False, stop=False, skip_group_check=True)
                return pe.matmul(out, sl, mh, start=False, stop=stop, skip_group_check=True)

            def experts(d, n, t):
                if t == 0:
                    if has(n):
                        after(pe, "roped", n, 1, 1)
                    else:
                        after(pe, "vrows_done", d + 2, 1, 1)
                else:
                    after(pe, "moe_taken", d, 2, 1)
                for h in range(2):
                    o = ps_m[:, h, :].rearrange("p (e f) -> p e f", e=4)
                    tok = slice(128 * t, 128 * t + 128)
                    three(o, (x1t_hi[:, tok], x1t_lo[:, tok]), (we_hi[:, 4 * h:4 * h + 4, :], we_lo[:, 4 * h:4 * h + 4, :]),
                          True, False)
                    if h == 0:
                        after(pe, "route_done", d, 1, 1)
                    mm = pe.matmul(ps_m[:, h, :], route[:, tok], route_rows[:, 512 * h:512 * h + 512],
                                   start=False, stop=True, skip_group_check=True)
                mm.then_inc(s_["moe_ready"], 1)

            def masks(dst, chunk, rows, at_end):
                blocks, groups = chunk
                starts = [sum(width(b) for b in blocks[:n]) + (width(j) - BLK if at_end else 0)
                          for n, j in enumerate(blocks)]
                v = dst[:, 0:columns_of(chunk)].rearrange("p (g x) -> p g x", g=len(groups))
                if len(blocks) == 1:
                    v = v[:, :, starts[0]:starts[0] + BLK]
                    rows = rows[:, :].unsqueeze(1).broadcast_to([128, len(groups), BLK])
                else:
                    apart = starts[1] - starts[0]
                    v = v.rearrange("p g (i x) -> p g i x", x=BLK)
                    v = v[:, :, starts[0] // BLK:starts[1] // BLK + 1:apart // BLK, :]
                    rows = rows[:, :].unsqueeze(1).unsqueeze(1).broadcast_to([128, len(groups), 2, BLK])
                return pe.matmul(v, ident_bf[:, :], rows, start=False, stop=True, skip_group_check=True)

            def step(s, p, half):
                n, a, b, c, d = s + 2, s + 1, s, s - 1, s - 2
                q = 1 - p
                for slot in range(SLOTS):
                    k = slot - B_SLOT
                    if has(c) and 0 <= k < NCH:
                        if k == 0:
                            after(pe, f"bops_loaded{q}", half(-1), OPS_LOADED, OPS_LOADED)
                            if is_step(s, 1):
                                pe.wait_ge(s_["start_act"], 3)
                            after(pe, "maxrows_loaded", c, 16, 16)
                        after(pe, "exp_done", c, NCH, k - 1)
                        for i, (j, g, col) in enumerate(parts_of(CHUNKS[k])):
                            pe.matmul(ps_b[k % 2][:, col:col + width(j)], diag_block(k_diag[q], g, j),
                                      q_plain[q][:, g, BLK * j:S], start=(i == 0), stop=False, skip_group_check=True)
                        masks(ps_b[k % 2], CHUNKS[k], mask_b_bf, False).then_inc(s_["b_ready"], 1)
                    t, k = maxima_at(slot, a, b)
                    if t is not None:
                        at = p if t is b else q
                        if k == 0:
                            after(pe, f"aops_loaded{at}", half(0 if t is b else 1), OPS_LOADED, OPS_LOADED)
                        after(pe, "a_taken", t, NCH, max(k - 1, 0))
                        for i, (j, g, col) in enumerate(parts_of(CHUNKS[k])):
                            pe.matmul(ps_a[k % 2][:, col:col + width(j)], diag_block(q_diag[at], g, NBLK - 1 - j),
                                      k_plain[at][:, g, 0:width(j)], start=(i == 0), stop=False, skip_group_check=True)
                        masks(ps_a[k % 2], CHUNKS[k], mask_a_bf, True).then_inc(s_["a_ready"], 1)
                    if slot == 13 and has(d):
                        experts(d, n, 1)
                    if slot == 11 and has(b):
                        after(pe, "parted", b, 2, 2)
                        if has(d):
                            after(pe, "route_done", d, 1, 1)
                        for i in range(NBLK // 4):
                            mm = pe.matmul(ps_n[:, BLK * i:BLK * i + BLK],
                                           max_parts[:, 4 * i:4 * i + 4, :].rearrange("p i m -> p (i m)"), stacked_r[:, :],
                                           start=(i == 0), stop=True, skip_group_check=True)
                        mm.then_inc(s_["ex_ready"], 1)
                    if slot == 12 and has(d):
                        experts(d, n, 0)
                    k = slot - PV_SLOT
                    if has(c) and 0 <= k < NCH:
                        after(pe, "exp_done", c, NCH, k + 1)
                        if k == 0:
                            after(pe, "v_done", c, 1, 1)
                            after(pe, "pv_copied", c)
                        for j, g, col in parts_of(CHUNKS[k]):
                            mm = pe.matmul(ps_pv[:, g // 2, BLK * j:S], v_diag[q][:, j, 128 * g:128 * g + 128],
                                           probs[:, k % PR, col:col + width(j)], start=(j == 0 and g == 0),
                                           stop=(k == NCH - 1), skip_group_check=True)
                        mm.then_inc(s_["pv_ready"], 1)
                    if slot == 4 and has(d):
                        after(pe, "normed", d, 1, 1)
                        after(pe, "maxrows_done", b)
                        for t in range(2):
                            mm = pe.matmul(ps_n[:, 128 * t:128 * t + 128], attn[:, 128 * t:128 * t + 128], wo_in[:, :],
                                           start=(t == 0), stop=True, skip_group_check=True)
                        mm.then_inc(s_["y_ready"], 1)
                    if slot == 7 and has(d):
                        after(pe, "x1_done", d, 2, 2)
                        for t in range(2):
                            mm = pe.transpose(ps_n[:, 128 * t:128 * t + 128], x1[:, t, :], C("ident"))
                        mm.then_inc(s_["x1t_ready"], 1)
                    if slot == 6 and has(b):
                        after(pe, "moe_taken", d - 1, 2, 2)
                        for t in range(2):
                            tok = slice(128 * t, 128 * t + 128)
                            mm = three(ps_m[:, 0, tok], (xt_hi[p][:, tok], xt_lo[p][:, tok]),
                                       (w_hi[:, 4, :], w_lo[:, 4, :]), t == 0, t == 1)
                        mm.then_inc(s_["v_ready"], 1)
                    if slot == 6 and has(n):
                        after(pe, "x_loaded", n, 16, 16)
                        after(pe, "moe_taken", d - 1, 2, 2)
                        for t in range(2):
                            mm = pe.transpose(ps_m[:, 1, 128 * t:128 * t + 128], x_in[:, t, :], C("ident"))
                        mm.then_inc(s_["xt_ready"], 1)
                    if slot == 9 and has(n):
                        after(pe, "xl_done", n, 1, 1)
                        if has(b):
                            after(pe, "vrows_done", b, 1, 1)
                        if is_step(s, -2):
                            pe.wait_ge(s_["w_split"], 2)
                        for i in range(2):
                            for o in range(2):
                                mm = three(ps_m[:, o, S * i:S * i + S], (w_hi[:, 2 * i + o, :], w_lo[:, 2 * i + o, :]),
                                           (xt_hi[p][:, :], xt_lo[p][:, :]), i == 0, i == 1)
                        mm.then_inc(s_["qk_ready"], 1)
                    if slot == 10 and is_step(s, -2):
                        start_late()
                    if slot == 11 and is_step(s, -1):
                        pe.wait_ge(s_["late_dve"], 7)
                    if slot == 8 and has(d):
                        after(pe, "x1l_done", d, 1, 1)
                        for t in range(2):
                            for i, xa in enumerate((x1t_hi, x1t_lo)):
                                mm = pe.matmul(ps_log[:, t], xa[:, 128 * t:128 * t + 128], wg_parts[:, :, :],
                                               start=(t == 0 and i == 0), stop=(i == 1), skip_group_check=True)
                        mm.then_inc(s_["logits_ready"], 1)
                    if slot == 10 and has(d):
                        after(pe, "chosen_done", d, 1, 1)
                        after(pe, "seen_done", d, 2)
                        pe.matmul(ps_loc, before_bf[:, :], chosen[:, :, :], start=True, stop=False, skip_group_check=True)
                        pe.matmul(ps_loc, ones_bf[:, :], seen[:, :].unsqueeze(1).broadcast_to([128, 2, E]),
                                  start=False, stop=False, skip_group_check=True)
                        pe.matmul(ps_loc[:, 1, :], ones_bf[:, :], chosen[:, 0, :], start=False, stop=True,
                                  skip_group_check=True)
                        for t in range(2):
                            mm = pe.transpose(ps_route[:, 128 * t:128 * t + 128], chosen_f[:, t, :], C("ident"))
                        mm.then_inc(s_["loc_ready"], 1)

            all_steps(pe, step)


def constants():
    c = np.zeros((128, NCONST), np.float32)
    def put(name, v, rows=slice(0, 128)):
        at, w = CONSTS[name]
        c[rows, at:at + w] = v
    p = np.arange(128)
    put("ident", np.eye(128))
    put("before", (p[:, None] < p[None, :]))
    inv_freq = (np.float32(1) / np.float32(10000) ** (np.arange(0, HD, 2, dtype=np.float32) / np.float32(HD))).astype(np.float32)
    freqs = (np.arange(S, dtype=np.float32)[None, :] * inv_freq[:, None]).astype(np.float32)
    rows = (p % HD) // 2
    put("cos", np.cos(freqs[rows].astype(np.float64)))
    put("sin", np.sin(freqs[rows].astype(np.float64)))
    r, col = p % BLK, np.arange(BLK)
    put("mask_a", np.where(col[None, :] > r[:, None], NEG, 0.0))
    put("mask_b", np.where(col[None, :] < r[:, None], NEG, 0.0))
    put("stacked", r[:, None] == col[None, :])
    put("head_cols", (p[:, None] // BLK) == ((p[None, :] // HD) % GH))
    put("head_is", (p[:, None] // BLK) == np.arange(GH)[None, :])
    put("tie", (E - np.arange(E))[None, :])
    put("max_sel", -((np.arange(32)[:, None] % H) == np.arange(H)[None, :]).astype(np.float32), slice(SCORE_ROWS, 128))
    sel = np.repeat(np.eye(E, dtype=np.float32), 128, axis=1)
    return c, sel


_INS = ['L0_attn_x', 'L0_attn_wq', 'L0_attn_bq', 'L0_attn_wk', 'L0_attn_bk', 'L0_attn_wv', 'L0_attn_bv', 'L0_attn_wo',
        'L0_attn_bo', 'L0_ffn_wg', 'L0_ffn_W', 'L0_ffn_b']


def kernel(**inputs):
    import numpy as _np
    import concourse.bacc as _bacc
    from concourse import mybir as _mybir
    from concourse.bass_utils import run_bass_kernel_spmd as _run

    nc = _bacc.Bacc("TRN2", target_bir_lowering=False, num_devices=1)
    arrays, args = {}, []
    for name in _INS:
        arrays[f"in_{name}_dram"] = _np.ascontiguousarray(inputs[name])
    table, sel = constants()
    arrays["in_table_dram"] = table
    arrays["in_expert_rows_dram"] = sel
    for name, a in arrays.items():
        args.append(nc.dram_tensor(name, a.shape, _mybir.dt.from_np(a.dtype), kind="ExternalInput").ap())
    args.append(nc.dram_tensor("out_0_dram", (B, S, D), _mybir.dt.float32, kind="ExternalOutput").ap())
    layer_kernel(nc, *args)
    r = _run(nc, [arrays], core_ids=[0])
    return r.results[0]["out_0_dram"]
```
